# Optimizing a Trainium2 kernel written in Bass

```python
import numpy as np
import jax
import jax.numpy as jnp

def _softmax(x, axis=-1):
    return jax.nn.softmax(x, axis=axis)

def _gelu(x):
    return jax.nn.gelu(x, approximate=True)

def _silu(x):
    return jax.nn.silu(x)

def _sigmoid(x):
    return jax.nn.sigmoid(x)

def _layernorm(x, axis=-1, eps=1e-05):
    m = jnp.mean(x, axis=axis, keepdims=True)
    v = jnp.var(x, axis=axis, keepdims=True)
    return (x - m) / jnp.sqrt(v + eps)

def _scatter_add(tgt, idx, src, axis=0):
    return tgt.at[idx].add(src)

def _segment_sum(src, seg, n):
    return jax.ops.segment_sum(src, seg, n)
kernel_name = 'mk_flamingo_gated_d1_seqx_r8_0f6a4c'

def setup_inputs(seed: int=0):
    np.random.seed(seed)
    _w = jnp.asarray

    def _rec_inputs():
        import jax
        import jax.numpy as jnp
        _rk = jax.random.key(seed)
        x = -0.000125 + 0.9999 * jax.random.normal(jax.random.fold_in(_rk, 1), (32, 64, 512), jnp.float32)
        _lenS = 64 - jax.random.randint(jax.random.fold_in(_rk, 7), (32,), 0, max(1, 64 // 4) + 1, jnp.int32)
        _lenS2 = 64 - jax.random.randint(jax.random.fold_in(_rk, 8), (32,), 0, max(1, 64 // 4) + 1, jnp.int32)
        _ctx_4096P = jax.random.normal(jax.random.fold_in(_rk, 11), (32, 16, 512), jnp.float32)
        _ctx_4096c = jax.random.dirichlet(jax.random.fold_in(_rk, 511), 0.3 * jnp.ones((16,), jnp.float32), (32, 64))
        _ctx_4096t = jnp.einsum('bsk,bkd->bsd', _ctx_4096c, _ctx_4096P)
        _ctx_4096t = _ctx_4096t * jax.lax.rsqrt(jnp.mean(jnp.square(_ctx_4096t)) + 1e-12) * 0.953939
        ctx_4096 = -1.52775e-05 + 0.999936 * (_ctx_4096t + 0.3 * jax.random.normal(jax.random.fold_in(_rk, 611), (32, 64, 512), jnp.float32))
        _g = jax.random.normal(jax.random.fold_in(_rk, 9001), (2, 1), jnp.float32)
        _g = jnp.sign(_g) * jnp.maximum(jnp.abs(_g), 1.0) + (_g == 0) * 1.0
        g_xattn = _g[0]
        g_ffn = _g[1]
        return (x, ctx_4096, g_xattn, g_ffn)
    x, ctx_4096, g_xattn, g_ffn = _rec_inputs()

    def _L0_xattn_setup():
        import jax, jax.numpy as jnp
        import numpy as np
        H = 8
        C = 2

        def _autocorrelation(Q, K, V):
            B, L, D = Q.shape
            d = D // H
            q = Q.reshape(B, L, H, d).transpose(0, 2, 1, 3)
            k = K.reshape(B, L, H, d).transpose(0, 2, 1, 3)
            v = V.reshape(B, L, H, d).transpose(0, 2, 1, 3)
            qf = jnp.fft.fft(q, axis=2)
            kf = jnp.fft.fft(k, axis=2)
            corr = jnp.fft.ifft(qf * jnp.conj(kf), axis=2).real
            topk = int(C * np.log(L))
            w, idx = jax.lax.top_k(corr.transpose(0, 1, 3, 2), topk)
            w = jax.nn.softmax(w, axis=-1)
            pos = jnp.arange(L)[:, None]
            out = jnp.zeros_like(v)
            for i in range(topk):
                g = jnp.minimum(idx[:, :, None, :, i] + pos, L - 1)
                out = out + w[:, :, None, :, i] * jnp.take_along_axis(v, g, axis=2)
            return out.transpose(0, 2, 1, 3).reshape(B, L, D)
        key = jax.random.key(seed)
        k1, k2, k3 = jax.random.split(key, 3)
        B, L, D = (16, 64, 512)
        Q = jax.random.normal(k1, (B, L, D), dtype=jnp.float32)
        K = jax.random.normal(k2, (B, L, D), dtype=jnp.float32)
        V = jax.random.normal(k3, (B, L, D), dtype=jnp.float32)
        return {'Q': Q, 'K': K, 'V': V}
    _L0_xattn_all = _L0_xattn_setup()
    _L0_xattn_in = {k: v for k, v in _L0_xattn_all.items() if k in ()}
    del _L0_xattn_all

    def _L0_ffn_setup():
        import jax, jax.numpy as jnp
        import numpy as np
        B, S, IN, OUT = (4, 256, 512, 512)
        E, K, R = (8, 2, 16)
        CAP_FACTOR = 3.0
        ALPHA = 1.0 / R
        LN_EPS = 1e-05
        key = jax.random.key(seed)
        ks = jax.random.split(key, 6)
        return {'x': jax.random.normal(ks[0], (B, S, IN), dtype=jnp.float32), 'weight': jax.random.normal(ks[1], (OUT, IN), dtype=jnp.float32) * 0.02, 'lora_A': jax.random.normal(ks[2], (E, IN, R), dtype=jnp.float32) / np.sqrt(R), 'lora_B': jax.random.normal(ks[3], (E, R, OUT), dtype=jnp.float32) * 0.02, 'gw1': jax.random.normal(ks[4], (4 * E, IN), dtype=jnp.float32) * 0.02, 'gb1': jnp.zeros((4 * E,), dtype=jnp.float32), 'ln_gamma': jnp.ones((4 * E,), dtype=jnp.float32), 'ln_beta': jnp.zeros((4 * E,), dtype=jnp.float32), 'gw2': jax.random.normal(ks[5], (E, 4 * E), dtype=jnp.float32) * 0.02, 'gb2': jnp.zeros((E,), dtype=jnp.float32)}
    _L0_ffn_all = _L0_ffn_setup()
    _L0_ffn_in = {k: v for k, v in _L0_ffn_all.items() if k in ('weight', 'lora_A', 'lora_B', 'gw1', 'gb1', 'ln_gamma', 'ln_beta', 'gw2', 'gb2')}
    del _L0_ffn_all
    return {'x': x, 'ctx_4096': ctx_4096, 'g_xattn': g_xattn, 'g_ffn': g_ffn, 'L0_ffn_weight': _L0_ffn_in['weight'], 'L0_ffn_lora_A': _L0_ffn_in['lora_A'], 'L0_ffn_lora_B': _L0_ffn_in['lora_B'], 'L0_ffn_gw1': _L0_ffn_in['gw1'], 'L0_ffn_gb1': _L0_ffn_in['gb1'], 'L0_ffn_ln_gamma': _L0_ffn_in['ln_gamma'], 'L0_ffn_ln_beta': _L0_ffn_in['ln_beta'], 'L0_ffn_gw2': _L0_ffn_in['gw2'], 'L0_ffn_gb2': _L0_ffn_in['gb2']}

def reference(x, ctx_4096, g_xattn, g_ffn, L0_ffn_weight, L0_ffn_lora_A, L0_ffn_lora_B, L0_ffn_gw1, L0_ffn_gb1, L0_ffn_ln_gamma, L0_ffn_ln_beta, L0_ffn_gw2, L0_ffn_gb2):
    import jax
    import jax.numpy as jnp

    def _L0_xattn_ref(Q, K, V):
        import jax, jax.numpy as jnp
        import numpy as np
        H = 8
        C = 2

        def _autocorrelation(Q, K, V):
            B, L, D = Q.shape
            d = D // H
            q = Q.reshape(B, L, H, d).transpose(0, 2, 1, 3)
            k = K.reshape(B, L, H, d).transpose(0, 2, 1, 3)
            v = V.reshape(B, L, H, d).transpose(0, 2, 1, 3)
            qf = jnp.fft.fft(q, axis=2)
            kf = jnp.fft.fft(k, axis=2)
            corr = jnp.fft.ifft(qf * jnp.conj(kf), axis=2).real
            topk = int(C * np.log(L))
            w, idx = jax.lax.top_k(corr.transpose(0, 1, 3, 2), topk)
            w = jax.nn.softmax(w, axis=-1)
            pos = jnp.arange(L)[:, None]
            out = jnp.zeros_like(v)
            for i in range(topk):
                g = jnp.minimum(idx[:, :, None, :, i] + pos, L - 1)
                out = out + w[:, :, None, :, i] * jnp.take_along_axis(v, g, axis=2)
            return out.transpose(0, 2, 1, 3).reshape(B, L, D)
        return _autocorrelation(Q, K, V)

    def _L0_ffn_ref(x, weight, lora_A, lora_B, gw1, gb1, ln_gamma, ln_beta, gw2, gb2):
        import jax, jax.numpy as jnp
        import numpy as np
        B, S, IN, OUT = (4, 256, 512, 512)
        E, K, R = (8, 2, 16)
        CAP_FACTOR = 3.0
        ALPHA = 1.0 / R
        LN_EPS = 1e-05
        orig_shape = x.shape
        xf = x.reshape(-1, orig_shape[-1])
        N = xf.shape[0]
        capacity = int(CAP_FACTOR * N / E)
        h = xf @ gw1.T + gb1
        mu = jnp.mean(h, axis=-1, keepdims=True)
        var = jnp.mean((h - mu) ** 2, axis=-1, keepdims=True)
        h = (h - mu) * jax.lax.rsqrt(var + LN_EPS) * ln_gamma + ln_beta
        h = jax.nn.relu(h)
        gates = h @ gw2.T + gb2
        top_v, top_i = jax.lax.top_k(gates, K)
        top_g = jax.nn.softmax(top_v, axis=-1)
        onehot = (top_i[..., None] == jnp.arange(E)).astype(xf.dtype)
        counts = onehot.sum(axis=0)
        allowed = (counts <= capacity).astype(xf.dtype)
        w = jnp.einsum('nke,nk,ke->ne', onehot, top_g, allowed)
        main = xf @ weight.T
        tmp = jnp.einsum('ni,eir->enr', xf, lora_A)
        tmp = tmp * w.T[:, :, None]
        lora = jnp.einsum('enr,ero->no', tmp, lora_B) * ALPHA
        out = main + lora
        return out.reshape(*orig_shape[:-1], weight.shape[0])
    x = x + jnp.tanh(g_xattn[0]) * _L0_xattn_ref(_layernorm(x, axis=-1), ctx_4096, ctx_4096)
    x = x + jnp.tanh(g_ffn[0]) * _L0_ffn_ref(_layernorm(x, axis=-1), L0_ffn_weight, L0_ffn_lora_A, L0_ffn_lora_B, L0_ffn_gw1, L0_ffn_gb1, L0_ffn_ln_gamma, L0_ffn_ln_beta, L0_ffn_gw2, L0_ffn_gb2)
    return x

_drawn_inputs = setup_inputs


def setup_inputs(seed=0):
    import zlib

    import numpy as np

    out = dict(_drawn_inputs(seed))
    spreads = {'L0_ffn_gb1': (0.0, 0.8),
     'L0_ffn_ln_gamma': (1.0, 0.6),
     'L0_ffn_ln_beta': (0.0, 0.8),
     'L0_ffn_gb2': (0.0, 0.59)}
    factors = {'L0_ffn_lora_A': 5.597, 'L0_ffn_lora_B': 5.611, 'L0_ffn_gw1': 6.471, 'L0_ffn_gw2': 6.224}
    for name, (base, spread) in spreads.items():
        noise = np.random.default_rng([zlib.crc32(name.encode()), seed]).standard_normal(out[name].shape)
        drawn = base * np.exp(spread * noise) if base else spread * noise
        out[name] = jnp.asarray(drawn.astype(out[name].dtype))
    for name, factor in factors.items():
        out[name] = (out[name] * factor).astype(out[name].dtype)
    return out
```

```python
from contextlib import ExitStack

import numpy as np

import concourse.bass as bass
from concourse import mybir

F32 = mybir.dt.float32
ALU = mybir.AluOpType
ACT = mybir.ActivationFunctionType
AX_X = mybir.AxisListType.X

L = 64
HALF = L // 2
D = 512
P = 128
BATCH = 32
TILES = BATCH * L // P
CHUNKS = D // P
E = 8
R = 16
G1 = 4 * E
ER = E * R
SMALL = ER + G1
CAPACITY = int(3.0 * BATCH * L / E)
LN_EPS = 1e-5
LOW = -3.0e38
GROUP = 4
GROUPS = TILES // GROUP
MATRICES = ["fwd_even", "ctx_even", "ctx_odd", "fwd_odd", "corr_same", "corr_swap",
            "out_even_same", "out_even_swap", "out_odd_same", "out_odd_swap", "identity"]


def transform_matrices():
    t = np.arange(L)
    f = np.arange(HALF)
    even = 2 * np.pi * np.outer(t, f) / L
    odd = 2 * np.pi * np.outer(t, 2 * f + 1) / (2 * L)
    sign = (-1.0) ** t

    def forward(real, imag):
        m = np.zeros((2, L, 2, 2, HALF))
        for b in range(2):
            m[b, :, 0, b, :] = real
            m[b, :, 1, b, :] = imag
        return m.reshape(P, P)

    def inverse(part0, part1):
        m = np.zeros((2, 2, HALF, 2, L))
        for b in range(2):
            m[0, b, :, b, :] = part0
            m[1, b, :, b, :] = part1
        return m.reshape(P, P)

    er, ei = np.cos(even), -np.sin(even)
    ei[:, 0] = sign
    ger = er.copy()
    ger[L - 1, 0] = 1.0 + L
    orr, oi = np.cos(odd), -np.sin(odd)
    gor, goi = orr.copy(), oi.copy()
    gor[L - 1] -= orr.sum(0)
    goi[L - 1] -= oi.sum(0)
    ec, es = np.cos(even).T / L, np.sin(even).T / L
    oc, os_ = np.cos(odd).T / L, np.sin(odd).T / L
    c0, c1 = 2 * ec, 2 * ec
    c0[0] = 0.0
    c1 = c1.copy()
    c1[0] = sign / L
    o0, o1 = ec.copy(), ec.copy()
    o0[0] = 0.5 / L
    o1[0] = 0.5 * sign / L
    out = [forward(er, ei), forward(ger, ei), forward(gor, goi), forward(orr, oi),
           inverse(c0, c1), inverse(2 * es, -2 * es),
           inverse(o0, o1), inverse(-es, es),
           inverse(oc, oc), inverse(-os_, os_), np.eye(P)]
    return np.ascontiguousarray(np.concatenate(out, axis=1).astype(np.float32))


def build(nc, x, ctx, mats, desc, g_xattn, g_ffn, weight_t, small_t, lora_b, gb1, gamma, beta, gw2, gb2, out):
    with ExitStack() as stack:
        def sb(name, shape):
            return stack.enter_context(nc.sbuf_tensor(name, shape, F32))

        def ps(name):
            return stack.enter_context(nc.psum_tensor(name, [P, 512], F32))

        def sem(name):
            return stack.enter_context(nc.semaphore(name))

        x_all = sb("x_all", [P, TILES, D])
        ctx_all = sb("ctx_all", [P, TILES, D])
        mat = sb("mat", [P, len(MATRICES), P])
        xn = sb("xn", [P, 2, D])
        v_even = sb("v_even", [P, 2, D])
        v_even_sw = sb("v_even_sw", [P, 2, D])
        v_odd = sb("v_odd", [P, 2, D])
        v_odd_sw = sb("v_odd_sw", [P, 2, D])
        prod_q = sb("prod_q", [P, 2, D])
        prod_w = sb("prod_w", [P, 4, D])
        top = sb("top", [P, 8, 8])
        rest = sb("rest", [P, 8, L])
        top_d = sb("top_d", [P, 8, 8])
        top_e = sb("top_e", [P, 8, 8])
        top_sum = sb("top_sum", [P, 8])
        top_ln = sb("top_ln", [P, 8])
        shift = sb("shift", [P, 8])
        corr_d = sb("corr_d", [P, 8, L])
        corr_e = sb("corr_e", [P, 8, L])
        w_lag = sb("w_lag", [P, 8, L])
        w_time = sb("w_time", [P, D])
        bn = sb("bn", [P, 2, 6])
        mv = sb("mv", [P, 2, 2])
        var_eps = sb("var_eps", [P, 2])
        rstd = sb("rstd", [P, 2])
        nmr = sb("nmr", [P, 2])
        scratch = sb("scratch", [P, 4])
        eps_c = sb("eps_c", [P, 1])
        neg_c = sb("neg_c", [P, 1])
        m_half = sb("m_half", [P, TILES])
        bn2 = sb("bn2", [P, TILES, 6])
        mean2 = sb("mean2", [P, TILES])
        diff2 = sb("diff2", [P, TILES])
        sq2 = sb("sq2", [P, TILES])
        var_eps2 = sb("var_eps2", [P, TILES])
        rstd2 = sb("rstd2", [P, TILES])
        nmr2 = sb("nmr2", [P, TILES])
        gates_raw = sb("gates_raw", [P, 2])
        gate_t = sb("gate_t", [P, 2])
        gate_r = sb("gate_r", [P, 1])
        w_main = sb("w_main", [P, CHUNKS, D])
        w_small = sb("w_small", [P, CHUNKS, SMALL])
        w_b = sb("w_b", [P, D])
        gb1_b = sb("gb1_b", [P, G1])
        gamma_b = sb("gamma_b", [P, G1])
        beta_b = sb("beta_b", [P, G1])
        gw2_b = sb("gw2_b", [P, E, G1])
        gb2_b = sb("gb2_b", [P, E])
        desc_b = sb("desc_b", [P, E])
        xn2 = sb("xn2", [P, 2, D])
        x_t = sb("x_t", [P, 2, D])
        small = sb("small", [P, TILES, SMALL])
        h = sb("h", [P, GROUP, G1])
        hs = sb("hs", [P, GROUP, G1])
        st = sb("st", [P, GROUP])
        mu = sb("mu", [P, GROUP])
        ve = sb("ve", [P, GROUP])
        hr = sb("hr", [P, GROUP])
        gprod = sb("gprod", [P, GROUP, E, G1])
        gate = sb("gate", [P, GROUP, E])
        gate2 = sb("gate2", [P, GROUP, E])
        eq = sb("eq", [P, GROUP, E])
        key = sb("key", [P, GROUP, E])
        m1 = sb("m1", [P, GROUP])
        m2 = sb("m2", [P, GROUP])
        kmax = sb("kmax", [P, GROUP])
        gd = sb("gd", [P, GROUP])
        ge = sb("ge", [P, GROUP])
        gs = sb("gs", [P, GROUP])
        p1 = sb("p1", [P, GROUP])
        p2 = sb("p2", [P, GROUP])
        onehot = sb("onehot", [P, TILES, 2, E])
        weighted = sb("weighted", [P, TILES, 2, E])
        ohsum = sb("ohsum", [P, 2, E])
        ones = sb("ones", [P, P])
        allowed = sb("allowed", [P, 2, E])
        w_exp = sb("w_exp", [P, TILES, E])
        scaled = sb("scaled", [P, 2, GROUP, ER])
        scaled_t = sb("scaled_t", [P, 2, GROUP * P])
        result = sb("result", [P, 2, D])

        b_even, b_odd, b_q, b_corr, b_turn, b_we, b_wo, b_out = [
            ps(n) for n in ("b_even", "b_odd", "b_q", "b_corr", "b_turn", "b_we", "b_wo", "b_out")]
        b_xt = [b_even, b_odd]
        b_small = [b_q, b_corr]
        b_main = [b_turn, b_we]
        b_st = b_wo
        b_lora = [b_even, b_odd]

        x_in = [sem("x_in0"), sem("x_in1")]
        ctx_in = [sem("ctx_in0"), sem("ctx_in1")]
        mats_a_in, mats_b_in, gates_in, params_in = sem("mats_a_in"), sem("mats_b_in"), sem("gates_in"), sem("params_in")
        consts_set = sem("consts_set")
        tanh_done, gate_r_done = sem("tanh_done"), sem("gate_r_done")
        bn_done, mv_done, var_done, rstd_done, nmr_done, xn_done = [
            sem(n) for n in ("bn_done", "mv_done", "var_done", "rstd_done", "nmr_done", "xn_done")]
        even_mm, odd_mm, q_mm, corr_mm, turn_mm, we_mm, wo_mm, out_mm = [
            sem(n) for n in ("even_mm", "odd_mm", "q_mm", "corr_mm", "turn_mm", "we_mm", "wo_mm", "out_mm")]
        even_ev, odd_ev, wt_ev = sem("even_ev"), sem("odd_ev"), sem("wt_ev")
        pq_done, pe_done, po_done = sem("pq_done"), sem("pe_done"), sem("po_done")
        top_done, rest_done, topd_done, tope_done, tsum_done, ln_done, shift_done, corrd_done, corre_done, wlag_done = [
            sem(n) for n in ("top_done", "rest_done", "topd_done", "tope_done", "tsum_done", "ln_done",
                             "shift_done", "corrd_done", "corre_done", "wlag_done")]
        mr_done = sem("mr_done")
        var2_chain = sem("var2_chain")
        x1_done, bn2_done, mv2_done, rstd2_done, pool2_chain = [
            sem(n) for n in ("x1_done", "bn2_done", "mv2_done", "rstd2_done", "pool2_chain")]
        xn2_done, xt_mm, xt_ev, small_mm, small_ev, main_mm, base_done = [
            sem(n) for n in ("xn2_done", "xt_mm", "xt_ev", "small_mm", "small_ev", "main_mm", "base_done")]
        gchain, gvar_ready, grstd_done, gdiff_ready, gexp_done = [
            sem(n) for n in ("gchain", "gvar_ready", "grstd_done", "gdiff_ready", "gexp_done")]
        ohsum_done, count_mm, allowed_done, wexp_chain, scaled_done, st_mm, st_ev, lora_mm, result_done = [
            sem(n) for n in ("ohsum_done", "count_mm", "allowed_done", "wexp_chain", "scaled_done",
                             "st_mm", "st_ev", "lora_mm", "result_done")]
        stored = [sem("stored0"), sem("stored1")]

        def m(name):
            return mat[:, MATRICES.index(name), :]

        def at(buf, i):
            if isinstance(i, int):
                return buf[:, i, :]
            return buf[:, bass.ds(i, 1), :].rearrange("p a d -> p (a d)")

        x_rows = x.rearrange("(n p) d -> n p d", p=P)
        ctx_rows = ctx.rearrange("(n p) d -> n p d", p=P)
        out_rows = out.rearrange("(n p) d -> n p d", p=P)

        def row(src, i):
            if isinstance(i, int):
                return src[i, :, :]
            return src[bass.ds(i, 1), :, :].rearrange("a p d -> (a p) d")

        def held(use):
            nc.vector.memset(scratch[:, use:use + 1], 0.0)

        def run_pairs(eng, step):
            step(0, 0, True, False)
            with eng.Fori(0, (TILES - 2) // 2) as r:
                step(r * 2 + 1, 1, True, True)
                step(r * 2 + 2, 0, True, True)
            step(TILES - 1, 1, True, True)
            step(TILES, 0, False, True)

        block = stack.enter_context(nc.Block())

        @block.sync
        def _(sp):
            def load(i, par, again):
                if again is not None:
                    sp.wait_ge(x_in[par], i // 2 * 16 if isinstance(i, int) else again * 16)
                    sp.wait_ge(ctx_in[par], i // 2 * 16 if isinstance(i, int) else again * 16)
                sp.dma_start(at(x_all, i), row(x_rows, i)).then_inc(x_in[par], 16)
                sp.dma_start(at(ctx_all, i), row(ctx_rows, i)).then_inc(ctx_in[par], 16)

            na = MATRICES.index("fwd_odd")
            sp.dma_start(at(x_all, 0), x_rows[0, :, :]).then_inc(x_in[0], 16)
            sp.dma_start(mat[:, 0:na, :], mats.rearrange("p (n m) -> p n m", m=P)[:, 0:na, :]).then_inc(mats_a_in, 16)
            sp.dma_start(at(ctx_all, 0), ctx_rows[0, :, :]).then_inc(ctx_in[0], 16)
            sp.dma_start(gates_raw[:, 0:1], g_xattn.rearrange("(a n) -> a n", a=1).broadcast_to([P, 1])).then_inc(gates_in, 16)
            sp.dma_start(gates_raw[:, 1:2], g_ffn.rearrange("(a n) -> a n", a=1).broadcast_to([P, 1])).then_inc(gates_in, 16)
            sp.dma_start(mat[:, na:, :], mats.rearrange("p (n m) -> p n m", m=P)[:, na:, :]).then_inc(mats_b_in, 16)
            load(1, 1, None)
            with sp.Fori(1, TILES // 2) as r:
                load(r * 2, 0, r)
                load(r * 2 + 1, 1, r)
            sp.dma_start(w_main[:], weight_t.rearrange("(c p) n -> p c n", p=P)).then_inc(params_in, 16)
            sp.dma_start(w_small[:], small_t.rearrange("(c p) n -> p c n", p=P)).then_inc(params_in, 16)
            sp.dma_start(w_b[:], lora_b).then_inc(params_in, 16)
            for dst, src, n in ((gb1_b, gb1, G1), (gamma_b, gamma, G1), (beta_b, beta, G1), (gb2_b, gb2, E), (desc_b, desc, E)):
                sp.dma_start(dst[:], src.rearrange("(a n) -> a n", a=1).broadcast_to([P, n])).then_inc(params_in, 16)
            sp.dma_start(gw2_b[:].rearrange("p e g -> p (e g)"),
                         gw2.rearrange("(a e) g -> a (e g)", a=1).broadcast_to([P, E * G1])).then_inc(params_in, 16)

            def store(n, par, k):
                if not isinstance(n, int):
                    n = sp.snap(n)
                sp.wait_ge(result_done, k)
                sp.dma_start(row(out_rows, n), result[:, par, :]).then_inc(stored[par], 16)

            store(0, 0, 1)
            store(1, 1, 2)
            with sp.Fori(1, TILES // 2) as r:
                store(r * 2, 0, r * 2 + 1)
                store(r * 2 + 1, 1, r * 2 + 2)
            sp.wait_ge(stored[0], 16 * (TILES // 2))
            sp.wait_ge(stored[1], 16 * (TILES // 2))

        PARAMS = 16 * 9

        @block.gpsimd
        def _(pool):
            nc.gpsimd.memset(m_half[:], -0.5).then_inc(consts_set, 1)
            nc.gpsimd.memset(ones[:], 1.0).then_inc(consts_set, 1)
            nc.gpsimd.memset(eps_c[:], LN_EPS).then_inc(consts_set, 1)
            nc.gpsimd.memset(neg_c[:], -1.0).then_inc(consts_set, 1)
            pool.wait_ge(consts_set, 4)

            def statistics(i, par, k, old):
                pool.wait_ge(mv_done, k)
                nc.gpsimd.tensor_tensor(var_eps[:, par:par + 1], mv[:, par, 1:2], eps_c[:], ALU.add).then_inc(var_done, 1)
                pool.wait_ge(var_done, k)
                nc.gpsimd.tensor_tensor(rstd[:, par:par + 1], var_eps[:, par:par + 1], m_half[:, 0:1], ALU.pow).then_inc(rstd_done, 1)
                pool.wait_ge(rstd_done, k)
                if old is not None:
                    pool.wait_ge(xn_done, old)
                nc.gpsimd.tensor_tensor(nmr[:, par:par + 1], mv[:, par, 0:1], rstd[:, par:par + 1], ALU.mult).then_inc(mr_done, 1)
                pool.wait_ge(mr_done, k)
                nc.gpsimd.tensor_tensor(nmr[:, par:par + 1], nmr[:, par:par + 1], neg_c[:], ALU.mult).then_inc(nmr_done, 1)

            statistics(0, 0, 1, None)
            statistics(1, 1, 2, None)
            with pool.Fori(1, TILES // 2) as r:
                statistics(r * 2, 0, r * 2 + 1, r * 2 - 1)
                statistics(r * 2 + 1, 1, r * 2 + 2, r * 2)

            pool.wait_ge(mv2_done, 4)
            nc.gpsimd.tensor_tensor(rstd2[:], var_eps2[:], m_half[:], ALU.pow).then_inc(pool2_chain, 1)
            pool.wait_ge(pool2_chain, 1)
            nc.gpsimd.tensor_tensor(nmr2[:], mean2[:], rstd2[:], ALU.mult).then_inc(pool2_chain, 1)
            pool.wait_ge(pool2_chain, 2)
            nc.gpsimd.tensor_scalar(nmr2[:], nmr2[:], -0.5, 1.0, ALU.mult, ALU.mult).then_inc(rstd2_done, 1)

            def gate_power(k):
                pool.wait_ge(gvar_ready, k)
                nc.gpsimd.tensor_tensor(hr[:], ve[:], m_half[:, 0:GROUP], ALU.pow).then_inc(grstd_done, 1)

            with pool.Fori(0, GROUPS) as g:
                gate_power(g + 1)

        @block.tensor
        def _(pe):
            def step(i, par, ahead, behind):
                if ahead:
                    pe.wait_ge(ctx_in[par], (i // 2 + 1) * 16 if isinstance(i, int) else (i + (2 - par)) * 8)
                    if isinstance(i, int) and i == 0:
                        pe.wait_ge(mats_a_in, 16)
                    else:
                        pe.wait_ge(even_ev, i)
                    pe.matmul(b_even[:], m("ctx_even"), at(ctx_all, i), start=True, stop=True).then_inc(even_mm, 1)
                    if behind:
                        pe.wait_ge(odd_ev, i)
                    pe.matmul(b_odd[:], m("ctx_odd"), at(ctx_all, i), start=True, stop=True).then_inc(odd_mm, 1)
                    pe.wait_ge(xn_done, i + 1)
                    if behind:
                        pe.wait_ge(pq_done, i * 2)
                    pe.matmul(b_q[:], m("fwd_even"), xn[:, par, :], start=True, stop=True).then_inc(q_mm, 1)
                else:
                    pass
                if isinstance(i, int) and i == 0:
                    pe.wait_ge(mats_b_in, 16)
                if behind:
                    pe.wait_ge(wlag_done, i)
                    for c in range(CHUNKS):
                        turn = pe.transpose(b_turn[:, c * P:(c + 1) * P],
                                            w_lag[:].rearrange("p j l -> p (j l)")[:, c * P:(c + 1) * P], m("identity"))
                    turn.then_inc(turn_mm, 1)
                if ahead:
                    pe.wait_ge(pq_done, i * 2 + 2)
                    for c in range(CHUNKS):
                        pe.matmul(b_corr[:, c * P:(c + 1) * P], prod_q[:, 0, c * P:(c + 1) * P], m("corr_same"), start=True, stop=False)
                        corr = pe.matmul(b_corr[:, c * P:(c + 1) * P], prod_q[:, 1, c * P:(c + 1) * P], m("corr_swap"), start=False, stop=True)
                    corr.then_inc(corr_mm, 1)
                if behind:
                    pe.wait_ge(wt_ev, i)
                    if not (isinstance(i, int) and i == 1):
                        pe.wait_ge(pe_done, i * 2 - 2)
                    pe.matmul(b_we[:], m("fwd_even"), w_time[:], start=True, stop=True).then_inc(we_mm, 1)
                    if not (isinstance(i, int) and i == 1):
                        pe.wait_ge(po_done, i * 2 - 2)
                    pe.matmul(b_wo[:], m("fwd_odd"), w_time[:], start=True, stop=True).then_inc(wo_mm, 1)
                    pe.wait_ge(pe_done, i * 2)
                    if not (isinstance(i, int) and i == 1):
                        pe.wait_ge(x1_done, i - 1)
                    pe.matmul(b_out[:], m("out_even_same"), prod_w[:, 0, :], start=True, stop=False)
                    pe.matmul(b_out[:], m("out_even_swap"), prod_w[:, 1, :], start=False, stop=False)
                    pe.wait_ge(po_done, i * 2)
                    pe.matmul(b_out[:], m("out_odd_same"), prod_w[:, 2, :], start=False, stop=False)
                    pe.matmul(b_out[:], m("out_odd_swap"), prod_w[:, 3, :], start=False, stop=True).then_inc(out_mm, 1)

            run_pairs(pe, step)

            def turn_tokens(n, par, first):
                pe.wait_ge(xn2_done, n + 1)
                if not first:
                    pe.wait_ge(xt_ev, n - 1)
                for c in range(CHUNKS):
                    turn = pe.transpose(b_xt[par][:, c * P:(c + 1) * P], xn2[:, par, c * P:(c + 1) * P], m("identity"))
                turn.then_inc(xt_mm, 1)

            def small_product(n, par, first):
                pe.wait_ge(xt_ev, n + 1)
                if not first:
                    pe.wait_ge(small_ev, n - 1)
                for c in range(CHUNKS):
                    mm = pe.matmul(b_small[par][:, 0:SMALL], x_t[:, par, c * P:(c + 1) * P], w_small[:, c, :],
                                   start=(c == 0), stop=(c == CHUNKS - 1))
                mm.then_inc(small_mm, 1)

            def main_product(n, par, first):
                if not first:
                    pe.wait_ge(base_done, n - 1)
                for c in range(CHUNKS):
                    mm = pe.matmul(b_main[par][:], x_t[:, par, c * P:(c + 1) * P], w_main[:, c, :],
                                   start=(c == 0), stop=(c == CHUNKS - 1))
                mm.then_inc(main_mm, 1)

            pe.wait_ge(params_in, PARAMS)
            turn_tokens(0, 0, True)
            small_product(0, 0, True)

            def tile(n, par, first, last):
                if not last:
                    turn_tokens(n + 1, 1 - par, first)
                main_product(n, par, first or (isinstance(n, int) and n == 1))
                if not last:
                    small_product(n + 1, 1 - par, first)

            tile(0, 0, True, False)
            tile(1, 1, False, False)
            with pe.Fori(1, TILES // 2 - 1) as r:
                tile(r * 2, 0, False, False)
                tile(r * 2 + 1, 1, False, False)
            tile(TILES - 2, 0, False, False)
            tile(TILES - 1, 1, False, True)

            pe.wait_ge(ohsum_done, 1)
            pe.matmul(b_out[:, 0:2 * E], ones[:], ohsum[:].rearrange("p k e -> p (k e)"), start=True, stop=True).then_inc(count_mm, 1)

            def lora_group(g, par, first, w_scaled, w_st, w_lora):
                pe.wait_ge(scaled_done, w_scaled)
                if not first:
                    pe.wait_ge(st_ev, w_st - 1)
                for j in range(GROUP):
                    turn = pe.transpose(b_st[:, j * P:(j + 1) * P], scaled[:, par, j, :], m("identity"))
                turn.then_inc(st_mm, 1)
                pe.wait_ge(st_ev, w_st)
                for j in range(GROUP):
                    if not (first and j < 2):
                        pe.wait_ge(result_done, w_lora + j)
                    pe.matmul(b_lora[j % 2][:], scaled_t[:, par, j * P:(j + 1) * P], w_b[:], start=True, stop=True).then_inc(lora_mm, 1)

            lora_group(0, 0, True, 1, 1, -1)
            lora_group(1, 1, False, 2, 2, GROUP - 1)
            with pe.Fori(1, GROUPS // 2) as r:
                lora_group(r * 2, 0, False, r * 2 + 1, r * 2 + 1, r * (2 * GROUP) - 1)
                lora_group(r * 2 + 1, 1, False, r * 2 + 2, r * 2 + 2, r * (2 * GROUP) + GROUP - 1)

        @block.scalar
        def _(act):
            act.wait_ge(gates_in, 32)
            nc.scalar.activation(gate_t[:], gates_raw[:], ACT.Tanh).then_inc(tanh_done, 1)
            nc.scalar.preload_act_table(ACT.Ln)

            def spectrum(dst, dst_sw, bank, par, ready, done, i, free):
                act.wait_ge(ready, i + 1)
                if free is not None:
                    act.wait_ge(free[0], free[1])
                nc.scalar.activation(dst[:, par, :], bank[:], ACT.Identity)
                nc.scalar.activation(dst_sw[0:L, par, :], bank[L:P, :], ACT.Identity)
                nc.scalar.activation(dst_sw[L:P, par, :], bank[0:L, :], ACT.Identity).then_inc(done, 1)

            def normalise(i, par, free):
                act.wait_ge(nmr_done, i + 1)
                if free is not None:
                    act.wait_ge(q_mm, free)
                nc.scalar.activation(xn[:, par, :], at(x_all, i), ACT.Identity, bias=nmr[:, par:par + 1],
                                     scale=rstd[:, par:par + 1]).then_inc(xn_done, 1)

            def step(i, par, ahead, behind):
                early = isinstance(i, int) and i < 2
                if isinstance(i, int) and i == 0:
                    normalise(0, 0, None)
                if ahead:
                    spectrum(v_even, v_even_sw, b_even, par, even_mm, even_ev, i, None if early else (pe_done, i * 2 - 2))
                if behind:
                    act.wait_ge(turn_mm, i)
                    if not (isinstance(i, int) and i == 1):
                        act.wait_ge(wo_mm, i - 1)
                    nc.scalar.activation(w_time[:], b_turn[:], ACT.Identity).then_inc(wt_ev, 1)
                if ahead:
                    spectrum(v_odd, v_odd_sw, b_odd, par, odd_mm, odd_ev, i, None if early else (po_done, i * 2 - 2))
                    if not (isinstance(i, int) and i == TILES - 1):
                        normalise(i + 1, 1 - par, i if behind else None)
                    act.wait_ge(topd_done, i + 1)
                    nc.scalar.activation(top_e[:], top_d[:], ACT.Exp).then_inc(tope_done, 1)
                    act.wait_ge(tsum_done, i + 1)
                    nc.scalar.activation(top_ln[:], top_sum[:], ACT.Ln).then_inc(ln_done, 1)
                    act.wait_ge(corrd_done, i + 1)
                    if behind:
                        act.wait_ge(wlag_done, i)
                    nc.scalar.activation(corr_e[:], corr_d[:], ACT.Exp).then_inc(corre_done, 1)

            run_pairs(act, step)

            act.wait_ge(rstd2_done, 1)

            def norm2(n, par, first):
                if not first:
                    act.wait_ge(xt_mm, n - 1)
                if isinstance(n, int):
                    s, b = rstd2[:, n:n + 1], nmr2[:, n:n + 1]
                else:
                    s, b = rstd2[:, bass.ds(n, 1)], nmr2[:, bass.ds(n, 1)]
                nc.scalar.activation(xn2[:, par, :], at(x_all, n), ACT.Identity, bias=b, scale=s).then_inc(xn2_done, 1)

            def token_copy(n, par, first):
                act.wait_ge(xt_mm, n + 1)
                if not first:
                    act.wait_ge(main_mm, n - 1)
                nc.scalar.activation(x_t[:, par, :], b_xt[par][:], ACT.Identity).then_inc(xt_ev, 1)

            norm2(0, 0, True)
            norm2(1, 1, True)
            token_copy(0, 0, True)

            def tile(n, par, first, last, k):
                if not last:
                    token_copy(n + 1, 1 - par, first)
                if k is not None:
                    norm2(n + 2, par, False)

            def gate_exp(k):
                act.wait_ge(gdiff_ready, k)
                nc.scalar.activation(ge[:], gd[:], ACT.Exp).then_inc(gexp_done, 1)

            for n in range(GROUP):
                tile(n, n % 2, n == 0, False, 1)
            with act.Fori(1, GROUPS - 1) as g:
                gate_exp(g)
                for j in range(GROUP):
                    tile(g * GROUP + j, j % 2, False, False, 1)
            gate_exp(GROUPS - 1)
            for n in range(TILES - GROUP, TILES):
                tile(n, n % 2, False, n == TILES - 1, 1 if n + 2 < TILES else None)
            gate_exp(GROUPS)

            def turned_copy(par, k, first):
                act.wait_ge(st_mm, k)
                if not first:
                    act.wait_ge(lora_mm, (k - 2) * GROUP)
                nc.scalar.activation(scaled_t[:, par, :], b_st[:], ACT.Identity).then_inc(st_ev, 1)

            turned_copy(0, 1, True)
            turned_copy(1, 2, True)
            with act.Fori(1, GROUPS // 2) as r:
                turned_copy(0, r * 2 + 1, False)
                turned_copy(1, r * 2 + 2, False)

        @block.vector
        def _(dve):
            def stats(i, par, k, free):
                dve.wait_ge(x_in[par], k)
                if free is not None:
                    dve.wait_ge(nmr_done, free)
                held(0)
                nc.vector.bn_stats(bn[:, par, :], at(x_all, i)).then_inc(bn_done, 1)
                dve.wait_ge(bn_done, i + 1)
                held(1)
                nc.vector.bn_aggr(mv[:, par, :], bn[:, par, :]).then_inc(mv_done, 1)

            def products(dst, first, bank, even, swapped, par, ready, done, i, free):
                dve.wait_ge(ready[0], i)
                dve.wait_ge(ready[1], i)
                if free is not None:
                    dve.wait_ge(free[0], free[1])
                nc.vector.tensor_tensor(dst[:, first, :], bank[:], even[:, par, :], ALU.mult).then_inc(done, 1)
                nc.vector.tensor_tensor(dst[:, first + 1, :], bank[:], swapped[:, par, :], ALU.mult).then_inc(done, 1)

            def step(i, par, ahead, behind):
                start = isinstance(i, int) and i == 0
                if ahead:
                    products(prod_q, 0, b_q, v_even, v_even_sw, par, (q_mm, even_ev), pq_done, i + 1,
                             (corr_mm, i) if behind else None)
                    if not (isinstance(i, int) and i == TILES - 1):
                        stats(i + 1, 1 - par, ((i + 1) // 2 + 1) * 16 if isinstance(i, int) else (i + (2 + par)) * 8,
                              i if behind else None)
                if behind:
                    late = None if isinstance(i, int) and i == 1 else (out_mm, i - 1)
                    products(prod_w, 0, b_we, v_even, v_even_sw, 1 - par, (we_mm, even_ev), pe_done, i, late)
                    products(prod_w, 2, b_wo, v_odd, v_odd_sw, 1 - par, (wo_mm, odd_ev), po_done, i, None)
                if ahead:
                    dve.wait_ge(corr_mm, i + 1)
                    held(2)
                    corr = b_corr[:].rearrange("p (j l) -> p j l", l=L)
                    for j in range(8):
                        best = nc.vector.max(top[:, j, :], corr[:, j, :])
                    best.then_inc(top_done, 1)
                    dve.wait_ge(top_done, i + 1)
                    if behind:
                        dve.wait_ge(tope_done, i)
                    nc.vector.tensor_tensor(top_d[:], top[:], top[:, :, 0:1].broadcast_to([P, 8, 8]), ALU.subtract).then_inc(topd_done, 1)
                    for j in range(8):
                        repl = nc.vector.match_replace(out=rest[:, j, :], in_to_replace=top[:, j, :], in_values=corr[:, j, :], imm_value=LOW)
                    repl.then_inc(rest_done, 1)
                    dve.wait_ge(tope_done, i + 1)
                    nc.vector.tensor_reduce(top_sum[:], top_e[:], AX_X, ALU.add).then_inc(tsum_done, 1)
                if behind:
                    dve.wait_ge(out_mm, i)
                    if start is False:
                        dve.wait_ge(tanh_done, 1)
                    nc.vector.scalar_tensor_tensor(out=at(x_all, i - 1), in0=b_out[:], scalar=gate_t[:, 0:1], in1=at(x_all, i - 1),
                                                   op0=ALU.mult, op1=ALU.add).then_inc(x1_done, 1)
                if ahead:
                    dve.wait_ge(ln_done, i + 1)
                    nc.vector.tensor_tensor(shift[:], top[:, :, 0], top_ln[:], ALU.add).then_inc(shift_done, 1)
                    dve.wait_ge(shift_done, i + 1)
                    nc.vector.tensor_tensor(corr_d[:], corr, shift[:].unsqueeze(2).broadcast_to([P, 8, L]), ALU.subtract).then_inc(corrd_done, 1)
                if behind:
                    dve.wait_ge(x1_done, i)
                    held(3)
                    nc.vector.bn_stats(at(bn2, i - 1), at(x_all, i - 1)).then_inc(bn2_done, 1)
                if ahead:
                    dve.wait_ge(rest_done, i + 1)
                    dve.wait_ge(corre_done, i + 1)
                    if behind:
                        dve.wait_ge(turn_mm, i)
                    nc.vector.scalar_tensor_tensor(out=w_lag[:], in0=rest[:], scalar=LOW, in1=corr_e[:],
                                                   op0=ALU.is_equal, op1=ALU.mult).then_inc(wlag_done, 1)

            stats(0, 0, 16, None)
            run_pairs(dve, step)

            dve.wait_ge(bn2_done, TILES)
            nc.vector.tensor_tensor(mean2[:], bn2[:, :, 1], bn2[:, :, 4], ALU.add).then_inc(mv2_done, 1)
            nc.vector.tensor_tensor(diff2[:], bn2[:, :, 1], bn2[:, :, 4], ALU.subtract)
            nc.vector.tensor_tensor(sq2[:], bn2[:, :, 2], bn2[:, :, 5], ALU.add).then_inc(mv2_done, 1)
            dve.wait_ge(mv2_done, 2)
            nc.vector.scalar_tensor_tensor(out=diff2[:], in0=diff2[:], scalar=0.25 * D, in1=diff2[:],
                                           op0=ALU.mult, op1=ALU.mult).then_inc(mv2_done, 1)
            dve.wait_ge(mv2_done, 3)
            nc.vector.tensor_tensor(diff2[:], diff2[:], sq2[:], ALU.add).then_inc(var2_chain, 1)
            dve.wait_ge(var2_chain, 1)
            nc.vector.tensor_scalar(var_eps2[:], diff2[:], 1.0 / D, LN_EPS, ALU.mult, ALU.add).then_inc(mv2_done, 1)
            nc.vector.tensor_scalar(gate_r[:], gate_t[:, 1:2], 1.0 / R, None, ALU.mult).then_inc(gate_r_done, 1)
            dve.wait_ge(params_in, PARAMS)

            def tile(n, par):
                dve.wait_ge(small_mm, n + 1)
                nc.vector.tensor_copy(at(small, n), b_small[par][:, 0:SMALL]).then_inc(small_ev, 1)
                dve.wait_ge(main_mm, n + 1)
                nc.vector.scalar_tensor_tensor(out=at(ctx_all, n), in0=b_main[par][:], scalar=gate_t[:, 1:2], in1=at(x_all, n),
                                               op0=ALU.mult, op1=ALU.add).then_inc(base_done, 1)

            LINKS = 28

            def gating(g, tiles, k, base):
                links = [0]

                def link(ins):
                    links[0] += 1
                    ins.then_inc(gchain, 1)
                    dve.wait_ge(gchain, base + links[0])

                hid = small[:, tiles, ER:SMALL]
                wide = [P, GROUP, G1]
                experts = [P, GROUP, E]

                def along(v, shape):
                    return v[:].unsqueeze(2).broadcast_to(shape)

                def over(v, shape):
                    return v[:].unsqueeze(1).broadcast_to(shape)

                dve.wait_ge(small_ev, k * GROUP)
                link(nc.vector.tensor_tensor(h[:], hid, over(gb1_b, wide), ALU.add))
                link(nc.vector.tensor_reduce(st[:], h[:], AX_X, ALU.add))
                link(nc.vector.tensor_scalar(mu[:], st[:], 1.0 / G1, None, ALU.mult))
                link(nc.vector.tensor_tensor(h[:], h[:], along(mu, wide), ALU.subtract))
                link(nc.vector.tensor_tensor(hs[:], h[:], h[:], ALU.mult))
                link(nc.vector.tensor_reduce(st[:], hs[:], AX_X, ALU.add))
                nc.vector.tensor_scalar(ve[:], st[:], 1.0 / G1, LN_EPS, ALU.mult, ALU.add).then_inc(gvar_ready, 1)
                dve.wait_ge(grstd_done, k)
                link(nc.vector.tensor_tensor(h[:], h[:], along(hr, wide), ALU.mult))
                link(nc.vector.tensor_tensor(h[:], h[:], over(gamma_b, wide), ALU.mult))
                link(nc.vector.tensor_tensor(h[:], h[:], over(beta_b, wide), ALU.add))
                link(nc.vector.tensor_scalar(h[:], h[:], 0.0, None, ALU.max))
                full = [P, GROUP, E, G1]
                link(nc.vector.tensor_tensor(gprod[:], h[:].unsqueeze(2).broadcast_to(full),
                                             gw2_b[:].unsqueeze(1).broadcast_to(full), ALU.mult))
                link(nc.vector.tensor_reduce(gate[:], gprod[:], AX_X, ALU.add))
                link(nc.vector.tensor_tensor(gate[:], gate[:], over(gb2_b, experts), ALU.add))

                def choose(values, top_value, k_th):
                    link(nc.vector.tensor_reduce(top_value[:], values[:], AX_X, ALU.max))
                    link(nc.vector.tensor_tensor(eq[:], values[:], along(top_value, experts), ALU.is_equal))
                    link(nc.vector.tensor_tensor(key[:], eq[:], over(desc_b, experts), ALU.mult))
                    link(nc.vector.tensor_reduce(kmax[:], key[:], AX_X, ALU.max))
                    link(nc.vector.tensor_tensor(onehot[:, tiles, k_th, :], key[:], along(kmax, experts), ALU.is_equal))

                choose(gate, m1, 0)
                link(nc.vector.scalar_tensor_tensor(out=gate2[:], in0=onehot[:, tiles, 0, :], scalar=LOW, in1=gate[:],
                                                    op0=ALU.mult, op1=ALU.add))
                choose(gate2, m2, 1)
                nc.vector.tensor_tensor(gd[:], m2[:], m1[:], ALU.subtract).then_inc(gdiff_ready, 1)
                dve.wait_ge(gexp_done, k)
                link(nc.vector.tensor_scalar(gs[:], ge[:], 1.0, None, ALU.add))
                link(nc.vector.reciprocal(p1[:], gs[:]))
                link(nc.vector.tensor_tensor(p2[:], ge[:], p1[:], ALU.mult))
                nc.vector.tensor_tensor(weighted[:, tiles, 0, :], onehot[:, tiles, 0, :], along(p1, experts), ALU.mult)
                nc.vector.tensor_tensor(weighted[:, tiles, 1, :], onehot[:, tiles, 1, :], along(p2, experts), ALU.mult).then_inc(gchain, 1)
                assert links[0] + 1 == LINKS, links

            with dve.Fori(0, GROUPS - 1) as g:
                for j in range(GROUP):
                    tile(g * GROUP + j, j % 2)
                gating(g, bass.ds(g * GROUP, GROUP), g + 1, g * LINKS)
            n = TILES - GROUP
            for j in range(GROUP):
                tile(n + j, j % 2)
            gating(GROUPS - 1, slice(n, TILES), GROUPS, (GROUPS - 1) * LINKS)

            dve.wait_ge(gchain, GROUPS * LINKS)
            nc.vector.tensor_reduce(ohsum[:], onehot[:].rearrange("p n k e -> p k e n"), AX_X, ALU.add).then_inc(ohsum_done, 1)
            dve.wait_ge(count_mm, 1)
            nc.vector.tensor_scalar(allowed[:].rearrange("p k e -> p (k e)"), b_out[:, 0:2 * E], float(CAPACITY), None, ALU.is_le).then_inc(allowed_done, 1)
            dve.wait_ge(allowed_done, 1)
            nc.vector.tensor_tensor(weighted[:], weighted[:], allowed[:].unsqueeze(1).broadcast_to([P, TILES, 2, E]), ALU.mult).then_inc(wexp_chain, 1)
            dve.wait_ge(wexp_chain, 1)
            nc.vector.tensor_tensor(w_exp[:], weighted[:, :, 0, :], weighted[:, :, 1, :], ALU.add).then_inc(wexp_chain, 1)
            dve.wait_ge(wexp_chain, 2)
            dve.wait_ge(gate_r_done, 1)

            def scale_group(tiles, par, free):
                if free is not None:
                    dve.wait_ge(st_mm, free)
                full = [P, GROUP, E, R]
                nc.vector.tensor_tensor(scaled[:, par, :, :].rearrange("p n (e r) -> p n e r", r=R),
                                        small[:, tiles, 0:ER].rearrange("p n (e r) -> p n e r", r=R),
                                        w_exp[:, tiles, :].unsqueeze(3).broadcast_to(full), ALU.mult).then_inc(scaled_done, 1)

            def finish(n, par, k, stored_before):
                dve.wait_ge(lora_mm, k)
                if stored_before is not None:
                    dve.wait_ge(stored[par], stored_before)
                nc.vector.scalar_tensor_tensor(out=result[:, par, :], in0=b_lora[par][:], scalar=gate_r[:, 0:1],
                                               in1=at(ctx_all, n), op0=ALU.mult, op1=ALU.add).then_inc(result_done, 1)

            scale_group(slice(0, GROUP), 0, None)
            scale_group(slice(GROUP, 2 * GROUP), 1, None)
            for n in range(GROUP):
                finish(n, n % 2, n + 1, n // 2 * 16 if n >= 2 else None)
            with dve.Fori(1, GROUPS - 1) as g:
                dve.wait_ge(st_mm, g)
                full = [P, GROUP, E, R]
                slot = (g + 1) % 2
                nc.vector.tensor_tensor(scaled[:, bass.ds(slot, 1), :, :].rearrange("p a n (e r) -> p (a n) e r", r=R),
                                        small[:, bass.ds(g * GROUP + GROUP, GROUP), 0:ER].rearrange("p n (e r) -> p n e r", r=R),
                                        w_exp[:, bass.ds(g * GROUP + GROUP, GROUP), :].unsqueeze(3).broadcast_to(full), ALU.mult).then_inc(scaled_done, 1)
                for j in range(GROUP):
                    finish(g * GROUP + j, j % 2, g * GROUP + j + 1, g * (GROUP // 2 * 16) + j // 2 * 16)
            for n in range(TILES - GROUP, TILES):
                finish(n, n % 2, n + 1, n // 2 * 16)


def kernel(**inputs):
    import concourse.bacc as bacc
    from concourse.bass_utils import run_bass_kernel_spmd as run

    def f(name):
        return np.ascontiguousarray(inputs[name])

    arrays = {
        "x": f("x").reshape(BATCH * L, D),
        "ctx": f("ctx_4096").reshape(BATCH * L, D),
        "mats": transform_matrices(),
        "desc": np.arange(E, 0, -1).astype(np.float32),
        "g_xattn": f("g_xattn"),
        "g_ffn": f("g_ffn"),
        "weight_t": np.ascontiguousarray(f("L0_ffn_weight").T),
        "small_t": np.ascontiguousarray(np.concatenate(
            [f("L0_ffn_lora_A").transpose(1, 0, 2).reshape(D, ER), f("L0_ffn_gw1").T], axis=1)),
        "lora_b": f("L0_ffn_lora_B").reshape(ER, D),
        "gb1": f("L0_ffn_gb1"),
        "gamma": f("L0_ffn_ln_gamma"),
        "beta": f("L0_ffn_ln_beta"),
        "gw2": f("L0_ffn_gw2"),
        "gb2": f("L0_ffn_gb2"),
    }
    nc = bacc.Bacc("TRN2", target_bir_lowering=False, num_devices=1)
    aps = [nc.dram_tensor(f"in_{n}", a.shape, F32, kind="ExternalInput").ap() for n, a in arrays.items()]
    out = nc.dram_tensor("out_x", (BATCH * L, D), F32, kind="ExternalOutput").ap()
    build(nc, *aps, out)
    r = run(nc, [{f"in_{n}": a for n, a in arrays.items()}], core_ids=[0])
    return r.results[0]["out_x"].reshape(BATCH, L, D)
```

```python
from contextlib import ExitStack

import numpy as np

import concourse.bass as bass
from concourse import mybir

F32 = mybir.dt.float32
ALU = mybir.AluOpType
ACT = mybir.ActivationFunctionType
AX_X = mybir.AxisListType.X

L = 64
HALF = L // 2
D = 512
P = 128
BATCH = 32
TILES = BATCH * L // P
CHUNKS = D // P
E = 8
R = 16
G1 = 4 * E
ER = E * R
SMALL = ER + G1
CAPACITY = int(3.0 * BATCH * L / E)
LN_EPS = 1e-5
LOW = -3.0e38
GROUP = 2
GROUPS = TILES // GROUP
LORA_GROUP = 4
LORA_GROUPS = TILES // LORA_GROUP
MATRICES = ["fwd_even", "ctx_even", "ctx_odd", "fwd_odd", "corr_same", "corr_swap",
            "out_even_same", "out_even_swap", "out_odd_same", "out_odd_swap", "identity"]


def transform_matrices():
    t = np.arange(L)
    f = np.arange(HALF)
    even = 2 * np.pi * np.outer(t, f) / L
    odd = 2 * np.pi * np.outer(t, 2 * f + 1) / (2 * L)
    sign = (-1.0) ** t

    def forward(real, imag):
        m = np.zeros((2, L, 2, 2, HALF))
        for b in range(2):
            m[b, :, 0, b, :] = real
            m[b, :, 1, b, :] = imag
        return m.reshape(P, P)

    def inverse(part0, part1):
        m = np.zeros((2, 2, HALF, 2, L))
        for b in range(2):
            m[0, b, :, b, :] = part0
            m[1, b, :, b, :] = part1
        return m.reshape(P, P)

    er, ei = np.cos(even), -np.sin(even)
    ei[:, 0] = sign
    ger = er.copy()
    ger[L - 1, 0] = 1.0 + L
    orr, oi = np.cos(odd), -np.sin(odd)
    gor, goi = orr.copy(), oi.copy()
    gor[L - 1] -= orr.sum(0)
    goi[L - 1] -= oi.sum(0)
    ec, es = np.cos(even).T / L, np.sin(even).T / L
    oc, os_ = np.cos(odd).T / L, np.sin(odd).T / L
    c0, c1 = 2 * ec, 2 * ec
    c0[0] = 0.0
    c1 = c1.copy()
    c1[0] = sign / L
    o0, o1 = ec.copy(), ec.copy()
    o0[0] = 0.5 / L
    o1[0] = 0.5 * sign / L
    out = [forward(er, ei), forward(ger, ei), forward(gor, goi), forward(orr, oi),
           inverse(c0, c1), inverse(2 * es, -2 * es),
           inverse(o0, o1), inverse(-es, es),
           inverse(oc, oc), inverse(-os_, os_), np.eye(P)]
    return np.ascontiguousarray(np.concatenate(out, axis=1).astype(np.float32))


def build(nc, x, ctx, mats, index, g_xattn, g_ffn, weight_t, small_t, lora_b, gb1, gamma, beta, gw2, gb2, out):
    with ExitStack() as stack:
        def sb(name, shape):
            return stack.enter_context(nc.sbuf_tensor(name, shape, F32))

        def ps(name):
            return stack.enter_context(nc.psum_tensor(name, [P, 512], F32))

        def sem(name):
            return stack.enter_context(nc.semaphore(name))

        x_all = sb("x_all", [P, TILES, D])
        ctx_all = sb("ctx_all", [P, TILES, D])
        mat = sb("mat", [P, len(MATRICES), P])
        xn = sb("xn", [P, 2, D])
        v_even = sb("v_even", [P, 2, D])
        v_even_sw = sb("v_even_sw", [P, 2, D])
        v_odd = sb("v_odd", [P, 2, D])
        v_odd_sw = sb("v_odd_sw", [P, 2, D])
        prod_q = sb("prod_q", [P, 2, D])
        prod_w = sb("prod_w", [P, 4, D])
        top = sb("top", [P, 8, 8])
        rest = sb("rest", [P, 8, L])
        top_d = sb("top_d", [P, 8, 8])
        top_e = sb("top_e", [P, 8, 8])
        top_sum = sb("top_sum", [P, 8])
        top_ln = sb("top_ln", [P, 8])
        shift = sb("shift", [P, 8])
        corr_d = sb("corr_d", [P, 8, L])
        corr_e = sb("corr_e", [P, 8, L])
        w_lag = sb("w_lag", [P, 8, L])
        w_time = sb("w_time", [P, D])
        bn = sb("bn", [P, 2, 6])
        mv = sb("mv", [P, 2, 2])
        var_eps = sb("var_eps", [P, 2])
        rstd = sb("rstd", [P, 2])
        nmr = sb("nmr", [P, 2])
        scratch = sb("scratch", [P, 12])
        pool_scratch = sb("pool_scratch", [P, 1])
        eps_c = sb("eps_c", [P, GROUP])
        neg_c = sb("neg_c", [P, 1])
        m_half = sb("m_half", [P, GROUP])
        bn2 = sb("bn2", [P, 2, 6])
        mv2 = sb("mv2", [P, 2, 2])
        var_eps2 = sb("var_eps2", [P, 2])
        rstd2 = sb("rstd2", [P, 2])
        nmr2 = sb("nmr2", [P, 2])
        gates_raw = sb("gates_raw", [P, 2])
        gate_t = sb("gate_t", [P, 2])
        gate_r = sb("gate_r", [P, 1])
        w_main = sb("w_main", [P, CHUNKS, D])
        w_small = sb("w_small", [P, CHUNKS, SMALL])
        w_b = sb("w_b", [P, D])
        gb1_b = sb("gb1_b", [P, G1])
        gamma_b = sb("gamma_b", [P, G1])
        beta_b = sb("beta_b", [P, G1])
        gw2_b = sb("gw2_b", [P, E, G1])
        gb2_b = sb("gb2_b", [P, E])
        index_b = sb("index_b", [P, E])
        xn2 = sb("xn2", [P, 2, D])
        wo_sb = sb("wo_sb", [P, D])
        main_g = sb("main_g", [P, D])
        x_t = sb("x_t", [P, D])
        small = sb("small", [P, TILES, SMALL])
        h = sb("h", [P, GROUP, G1])
        bn_h = sb("bn_h", [P, GROUP, 6])
        mv_h = sb("mv_h", [P, GROUP, 2])
        ve = sb("ve", [P, GROUP])
        hr = sb("hr", [P, GROUP])
        gprod = sb("gprod", [P, GROUP, E, G1])
        gate = sb("gate", [P, GROUP, E])
        best = sb("best", [P, GROUP, E])
        best_at = stack.enter_context(nc.sbuf_tensor("best_at", [P, GROUP, E], mybir.dt.uint32))
        gd = sb("gd", [P, GROUP])
        ge = sb("ge", [P, GROUP])
        gs = sb("gs", [P, GROUP])
        p_top = sb("p_top", [P, GROUP, 2])
        onehot = sb("onehot", [P, TILES, 2, E])
        weighted = sb("weighted", [P, TILES, 2, E])
        ohsum = sb("ohsum", [P, 2, E])
        ones = sb("ones", [P, P])
        allowed = sb("allowed", [P, 2, E])
        w_exp = sb("w_exp", [P, TILES, E])
        scaled = sb("scaled", [P, LORA_GROUPS, LORA_GROUP, ER])
        scaled_t = sb("scaled_t", [P, TILES * P])

        b_even, b_odd, b_q, b_corr, b_turn, b_we, b_wo, b_out = [
            ps(n) for n in ("b_even", "b_odd", "b_q", "b_corr", "b_turn", "b_we", "b_wo", "b_out")]
        b_xt = b_small = b_even
        b_main = b_turn
        b_st = [b_wo, b_we, b_turn, b_corr]
        b_lora = [b_even, b_odd, b_q, b_out]

        x_in = [sem("x_in0"), sem("x_in1")]
        ctx_in = [sem("ctx_in0"), sem("ctx_in1")]
        mats_a_in, mats_b_in, gates_in, params_in = sem("mats_a_in"), sem("mats_b_in"), sem("gates_in"), sem("params_in")
        consts_set = sem("consts_set")
        tanh_done, gate_r_done = sem("tanh_done"), sem("gate_r_done")
        bn_done, mv_done, var_done, rstd_done, nmr_done, xn_done = [
            sem(n) for n in ("bn_done", "mv_done", "var_done", "rstd_done", "nmr_done", "xn_done")]
        even_mm, odd_mm, q_mm, corr_mm, turn_mm, we_mm, wo_mm, out_mm = [
            sem(n) for n in ("even_mm", "odd_mm", "q_mm", "corr_mm", "turn_mm", "we_mm", "wo_mm", "out_mm")]
        even_ev, odd_ev, wt_ev = sem("even_ev"), sem("odd_ev"), sem("wt_ev")
        pq_done, pe_done, po_done = sem("pq_done"), sem("pe_done"), sem("po_done")
        top_done, rest_done, topd_done, tope_done, tsum_done, ln_done, shift_done, corrd_done, corre_done, wlag_done = [
            sem(n) for n in ("top_done", "rest_done", "topd_done", "tope_done", "tsum_done", "ln_done",
                             "shift_done", "corrd_done", "corre_done", "wlag_done")]
        wo_ev, po_sw_done, main_ev, pool_held = sem("wo_ev"), sem("po_sw_done"), sem("main_ev"), sem("pool_held")
        gve_done = sem("gve_done")
        mr_done = sem("mr_done")
        x1_done, bn2_done, mv2_done, var2_done, rstd2_done, mr2_done, nmr2_done = [
            sem(n) for n in ("x1_done", "bn2_done", "mv2_done", "var2_done", "rstd2_done", "mr2_done", "nmr2_done")]
        xn2_done, xt_mm, xt_ev, small_mm, small_ev, main_mm, base_done = [
            sem(n) for n in ("xn2_done", "xt_mm", "xt_ev", "small_mm", "small_ev", "main_mm", "base_done")]
        gchain, gvar_ready, grstd_done, gdiff_ready, gexp_done = [
            sem(n) for n in ("gchain", "gvar_ready", "grstd_done", "gdiff_ready", "gexp_done")]
        ohsum_done, count_mm, allowed_done, wexp_chain, scaled_done, st_mm, st_ev, lora_mm, result_done = [
            sem(n) for n in ("ohsum_done", "count_mm", "allowed_done", "wexp_chain", "scaled_done",
                             "st_mm", "st_ev", "lora_mm", "result_done")]
        stored = [sem("stored0"), sem("stored1")]

        def m(name):
            return mat[:, MATRICES.index(name), :]

        def at(buf, i):
            if isinstance(i, int):
                return buf[:, i, :]
            return buf[:, bass.ds(i, 1), :].rearrange("p a d -> p (a d)")

        x_rows = x.rearrange("(n p) d -> n p d", p=P)
        ctx_rows = ctx.rearrange("(n p) d -> n p d", p=P)
        out_rows = out.rearrange("(n p) d -> n p d", p=P)

        def row(src, i):
            if isinstance(i, int):
                return src[i, :, :]
            return src[bass.ds(i, 1), :, :].rearrange("a p d -> (a p) d")

        def held(use):
            nc.vector.memset(scratch[:, use:use + 1], 0.0)

        def run_steps(eng, step):
            step(0, 0, True, False, False, False, None)
            step(1, 1, True, True, False, False, None)
            step(2, 0, True, True, True, False, None)
            step(3, 1, True, True, True, True, None)
            with eng.Fori(1, TILES // 2 - 2) as r:
                step(r * 2 + 2, 0, True, True, True, True, r - 1)
                step(r * 2 + 3, 1, True, True, True, True, r - 1)
            step(TILES - 2, 0, True, True, True, True, GROUPS - 3)
            step(TILES - 1, 1, True, True, True, True, GROUPS - 3)
            step(TILES, 0, False, True, True, True, GROUPS - 2)
            step(TILES + 1, 1, False, False, True, True, GROUPS - 2)
            step(TILES + 2, 0, False, False, False, True, GROUPS - 1)

        def is_step(i, n):
            return isinstance(i, int) and i == n

        block = stack.enter_context(nc.Block())

        @block.sync
        def _(sp):
            def load(i, par, again):
                if again is not None:
                    sp.wait_ge(x_in[par], i // 2 * 16 if isinstance(i, int) else again * 16)
                    sp.wait_ge(ctx_in[par], i // 2 * 16 if isinstance(i, int) else again * 16)
                sp.dma_start(at(x_all, i), row(x_rows, i)).then_inc(x_in[par], 16)
                sp.dma_start(at(ctx_all, i), row(ctx_rows, i)).then_inc(ctx_in[par], 16)

            na = MATRICES.index("fwd_odd")
            sp.dma_start(at(x_all, 0), x_rows[0, :, :]).then_inc(x_in[0], 16)
            sp.dma_start(mat[:, 0:na, :], mats.rearrange("p (n m) -> p n m", m=P)[:, 0:na, :]).then_inc(mats_a_in, 16)
            sp.dma_start(at(ctx_all, 0), ctx_rows[0, :, :]).then_inc(ctx_in[0], 16)
            sp.dma_start(gates_raw[:, 0:1], g_xattn.rearrange("(a n) -> a n", a=1).broadcast_to([P, 1])).then_inc(gates_in, 16)
            sp.dma_start(gates_raw[:, 1:2], g_ffn.rearrange("(a n) -> a n", a=1).broadcast_to([P, 1])).then_inc(gates_in, 16)
            sp.dma_start(mat[:, na:, :], mats.rearrange("p (n m) -> p n m", m=P)[:, na:, :]).then_inc(mats_b_in, 16)
            load(1, 1, None)
            with sp.Fori(1, TILES // 2) as r:
                load(r * 2, 0, r)
                load(r * 2 + 1, 1, r)
            sp.dma_start(w_main[:], weight_t.rearrange("(c p) n -> p c n", p=P)).then_inc(params_in, 16)
            sp.dma_start(w_small[:], small_t.rearrange("(c p) n -> p c n", p=P)).then_inc(params_in, 16)
            sp.dma_start(w_b[:], lora_b).then_inc(params_in, 16)
            for dst, src, n in ((gb1_b, gb1, G1), (gamma_b, gamma, G1), (beta_b, beta, G1), (gb2_b, gb2, E), (index_b, index, E)):
                sp.dma_start(dst[:], src.rearrange("(a n) -> a n", a=1).broadcast_to([P, n])).then_inc(params_in, 16)
            sp.dma_start(gw2_b[:].rearrange("p e g -> p (e g)"),
                         gw2.rearrange("(a e) g -> a (e g)", a=1).broadcast_to([P, E * G1])).then_inc(params_in, 16)

            for n in range(TILES):
                sp.wait_ge(result_done, n + 1)
                sp.dma_start(out_rows[n, :, :], ctx_all[:, n, :]).then_inc(stored[n % 2], 16)
            sp.wait_ge(stored[0], 16 * (TILES // 2))
            sp.wait_ge(stored[1], 16 * (TILES // 2))

        PARAMS = 16 * 9

        @block.gpsimd
        def _(pool):
            nc.gpsimd.memset(m_half[:], -0.5).then_inc(consts_set, 1)
            nc.gpsimd.memset(ones[:], 1.0).then_inc(consts_set, 1)
            nc.gpsimd.memset(eps_c[:], LN_EPS).then_inc(consts_set, 1)
            nc.gpsimd.memset(neg_c[:], -1.0).then_inc(consts_set, 1)
            pool.wait_ge(consts_set, 4)

            def powers(stat, k, par, ve_, rs_, nm_, ready, sems):
                var_s, rs_s, mr_s, nm_s = sems
                col = slice(par, par + 1)
                pool.wait_ge(ready, k)
                nc.gpsimd.tensor_tensor(ve_[:, col], stat[:, par, 1:2], eps_c[:, 0:1], ALU.add).then_inc(var_s, 1)
                pool.wait_ge(var_s, k)
                nc.gpsimd.tensor_tensor(rs_[:, col], ve_[:, col], m_half[:, 0:1], ALU.pow).then_inc(rs_s, 1)
                pool.wait_ge(rs_s, k)
                nc.gpsimd.tensor_tensor(nm_[:, col], stat[:, par, 0:1], rs_[:, col], ALU.mult).then_inc(mr_s, 1)
                pool.wait_ge(mr_s, k)
                nc.gpsimd.tensor_tensor(nm_[:, col], nm_[:, col], neg_c[:], ALU.mult).then_inc(nm_s, 1)

            def gate_powers(k):
                pool.wait_ge(gvar_ready, k)
                nc.gpsimd.tensor_tensor(ve[:], mv_h[:, :, 1], eps_c[:], ALU.add).then_inc(gve_done, 1)
                pool.wait_ge(gve_done, k)
                nc.gpsimd.tensor_tensor(hr[:], ve[:], m_half[:], ALU.pow).then_inc(grstd_done, 1)

            def step(i, par, ahead, behind, norm, ffn, group):
                if is_step(i, 0):
                    powers(mv, 1, 0, var_eps, rstd, nmr, mv_done, (var_done, rstd_done, mr_done, nmr_done))
                if norm:
                    if not is_step(i, 2) and not is_step(i, 3):
                        pool.wait_ge(xn2_done, i - 3)
                    powers(mv2, i - 1, par, var_eps2, rstd2, nmr2, mv2_done, (var2_done, rstd2_done, mr2_done, nmr2_done))
                if ahead and not is_step(i, TILES - 1):
                    if behind:
                        pool.wait_ge(xn_done, i)
                    powers(mv, i + 2, 1 - par, var_eps, rstd, nmr, mv_done, (var_done, rstd_done, mr_done, nmr_done))
                if behind:
                    pool.wait_ge(wo_ev, i)
                    pool.wait_ge(odd_ev, i)
                    if not is_step(i, 1):
                        pool.wait_ge(out_mm, i - 1)
                    nc.gpsimd.tensor_tensor(prod_w[:, 3, :], wo_sb[:], v_odd_sw[:, 1 - par, :], ALU.mult).then_inc(po_sw_done, 1)
                if ffn:
                    pool.wait_ge(main_ev, i - 2)
                    nc.gpsimd.tensor_tensor(pool_scratch[:], eps_c[:, 0:1], neg_c[:], ALU.mult).then_inc(pool_held, 1)
                    nc.gpsimd.tensor_tensor(at(ctx_all, i - 3), main_g[:], at(x_all, i - 3), ALU.add).then_inc(base_done, 1)
                if group is not None and par == 0:
                    gate_powers(group + 1)

            run_steps(pool, step)

        @block.tensor
        def _(pe):
            def step(i, par, ahead, behind, norm, ffn, group):
                if ahead:
                    pe.wait_ge(ctx_in[par], (i // 2 + 1) * 16 if isinstance(i, int) else (i + (2 - par)) * 8)
                    if not behind:
                        pe.wait_ge(mats_a_in, 16)
                    else:
                        pe.wait_ge(even_ev, i)
                    if ffn and not is_step(i, 3):
                        pe.wait_ge(small_ev, i - 3)
                    pe.matmul(b_even[:], m("ctx_even"), at(ctx_all, i), start=True, stop=True).then_inc(even_mm, 1)
                    pe.wait_ge(xn_done, i + 1)
                    if behind:
                        pe.wait_ge(pq_done, i * 2)
                    pe.matmul(b_q[:], m("fwd_even"), xn[:, par, :], start=True, stop=True).then_inc(q_mm, 1)
                if not behind and ahead:
                    pe.wait_ge(mats_b_in, 16)
                if behind:
                    pe.wait_ge(wlag_done, i)
                    if ffn and not is_step(i, 3):
                        pe.wait_ge(main_ev, i - 3)
                    for c in range(CHUNKS):
                        turn = pe.transpose(b_turn[:, c * P:(c + 1) * P],
                                            w_lag[:].rearrange("p j l -> p (j l)")[:, c * P:(c + 1) * P], m("identity"))
                    turn.then_inc(turn_mm, 1)
                if ahead:
                    if behind:
                        pe.wait_ge(odd_ev, i)
                    pe.matmul(b_odd[:], m("ctx_odd"), at(ctx_all, i), start=True, stop=True).then_inc(odd_mm, 1)
                if ffn:
                    pe.wait_ge(xn2_done, i - 2)
                    if ahead:
                        pe.wait_ge(even_ev, i + 1)
                    elif not is_step(i, TILES):
                        pe.wait_ge(small_ev, i - 3)
                    for c in range(CHUNKS):
                        turn = pe.transpose(b_xt[:, c * P:(c + 1) * P], xn2[:, 1 - par, c * P:(c + 1) * P], m("identity"))
                    turn.then_inc(xt_mm, 1)
                if behind:
                    pe.wait_ge(wt_ev, i)
                    if not is_step(i, 1):
                        pe.wait_ge(pe_done, i * 2 - 2)
                    pe.matmul(b_we[:], m("fwd_even"), w_time[:], start=True, stop=True).then_inc(we_mm, 1)
                    if not is_step(i, 1):
                        pe.wait_ge(po_done, i - 1)
                        pe.wait_ge(wo_ev, i - 1)
                    pe.matmul(b_wo[:], m("fwd_odd"), w_time[:], start=True, stop=True).then_inc(wo_mm, 1)
                if ffn:
                    if is_step(i, 3):
                        pe.wait_ge(params_in, PARAMS)
                    pe.wait_ge(xt_ev, i - 2)
                    for c in range(CHUNKS):
                        mm = pe.matmul(b_small[:, 0:SMALL], x_t[:, c * P:(c + 1) * P], w_small[:, c, :],
                                       start=(c == 0), stop=(c == CHUNKS - 1))
                    mm.then_inc(small_mm, 1)
                if ahead:
                    pe.wait_ge(pq_done, i * 2 + 2)
                    for c in range(CHUNKS):
                        pe.matmul(b_corr[:, c * P:(c + 1) * P], prod_q[:, 0, c * P:(c + 1) * P], m("corr_same"), start=True, stop=False)
                        corr = pe.matmul(b_corr[:, c * P:(c + 1) * P], prod_q[:, 1, c * P:(c + 1) * P], m("corr_swap"), start=False, stop=True)
                    corr.then_inc(corr_mm, 1)
                if ffn:
                    if not behind:
                        pe.wait_ge(main_ev, i - 3)
                    for c in range(CHUNKS):
                        mm = pe.matmul(b_main[:], x_t[:, c * P:(c + 1) * P], w_main[:, c, :],
                                       start=(c == 0), stop=(c == CHUNKS - 1))
                    mm.then_inc(main_mm, 1)
                if behind:
                    pe.wait_ge(pe_done, i * 2)
                    if not is_step(i, 1):
                        pe.wait_ge(x1_done, i - 1)
                    pe.matmul(b_out[:], m("out_even_same"), prod_w[:, 0, :], start=True, stop=False)
                    pe.matmul(b_out[:], m("out_even_swap"), prod_w[:, 1, :], start=False, stop=False)
                    pe.wait_ge(po_done, i)
                    pe.wait_ge(po_sw_done, i)
                    pe.matmul(b_out[:], m("out_odd_same"), prod_w[:, 2, :], start=False, stop=False)
                    pe.matmul(b_out[:], m("out_odd_swap"), prod_w[:, 3, :], start=False, stop=True).then_inc(out_mm, 1)

            run_steps(pe, step)

            pe.wait_ge(ohsum_done, 1)
            pe.matmul(b_out[:, 0:2 * E], ones[:], ohsum[:].rearrange("p k e -> p (k e)"), start=True, stop=True).then_inc(count_mm, 1)

            for g in range(LORA_GROUPS):
                pe.wait_ge(scaled_done, g + 1)
                if b_st[g] is b_main:
                    pe.wait_ge(main_ev, TILES)
                for j in range(LORA_GROUP):
                    turn = pe.transpose(b_st[g][:, j * P:(j + 1) * P], scaled[:, g, j, :], m("identity"))
                turn.then_inc(st_mm, 1)
            for n in range(TILES):
                if n % LORA_GROUP == 0:
                    pe.wait_ge(st_ev, n // LORA_GROUP + 1)
                if n >= LORA_GROUP:
                    pe.wait_ge(result_done, n - LORA_GROUP + 1)
                pe.matmul(b_lora[n % LORA_GROUP][:], scaled_t[:, n * P:(n + 1) * P], w_b[:], start=True, stop=True).then_inc(lora_mm, 1)

        @block.scalar
        def _(act):
            act.wait_ge(gates_in, 32)
            nc.scalar.activation(gate_t[:], gates_raw[:], ACT.Tanh).then_inc(tanh_done, 1)
            nc.scalar.preload_act_table_set("natural_log_exp_and_others")

            def spectrum(dst, dst_sw, bank, par, ready, done, i, free):
                act.wait_ge(ready, i + 1)
                for reader, count in free:
                    act.wait_ge(reader, count)
                nc.scalar.activation(dst[:, par, :], bank[:], ACT.Identity)
                nc.scalar.activation(dst_sw[0:L, par, :], bank[L:P, :], ACT.Identity)
                nc.scalar.activation(dst_sw[L:P, par, :], bank[0:L, :], ACT.Identity).then_inc(done, 1)

            def normalise(i, par, free):
                act.wait_ge(nmr_done, i + 1)
                if free is not None:
                    act.wait_ge(q_mm, free)
                nc.scalar.activation(xn[:, par, :], at(x_all, i), ACT.Identity, bias=nmr[:, par:par + 1],
                                     scale=rstd[:, par:par + 1]).then_inc(xn_done, 1)

            def gate_exp(group):
                act.wait_ge(gdiff_ready, group + 1)
                nc.scalar.activation(ge[:], gd[:], ACT.Exp).then_inc(gexp_done, 1)

            def step(i, par, ahead, behind, norm, ffn, group):
                early = isinstance(i, int) and i < 2
                if is_step(i, 0):
                    normalise(0, 0, None)
                if ahead:
                    spectrum(v_even, v_even_sw, b_even, par, even_mm, even_ev, i, () if early else ((pe_done, i * 2 - 2),))
                if behind:
                    act.wait_ge(turn_mm, i)
                    if not is_step(i, 1):
                        act.wait_ge(wo_mm, i - 1)
                    nc.scalar.activation(w_time[:], b_turn[:], ACT.Identity).then_inc(wt_ev, 1)
                if ffn:
                    act.wait_ge(xt_mm, i - 2)
                    if not is_step(i, 3):
                        act.wait_ge(main_mm, i - 3)
                    nc.scalar.activation(x_t[:], b_xt[:], ACT.Identity).then_inc(xt_ev, 1)
                if ahead:
                    spectrum(v_odd, v_odd_sw, b_odd, par, odd_mm, odd_ev, i, () if early else ((po_done, i - 1), (po_sw_done, i - 1)))
                if behind:
                    act.wait_ge(wo_mm, i)
                    if not is_step(i, 1):
                        act.wait_ge(po_sw_done, i - 1)
                    nc.scalar.activation(wo_sb[:], b_wo[:], ACT.Identity).then_inc(wo_ev, 1)
                if norm:
                    act.wait_ge(nmr2_done, i - 1)
                    if not is_step(i, 2) and not is_step(i, 3):
                        act.wait_ge(xt_mm, i - 3)
                    nc.scalar.activation(xn2[:, par, :], at(x_all, i - 2), ACT.Identity, bias=nmr2[:, par:par + 1],
                                         scale=rstd2[:, par:par + 1]).then_inc(xn2_done, 1)
                if ffn:
                    act.wait_ge(small_mm, i - 2)
                    nc.scalar.activation(at(small, i - 3), b_small[:, 0:SMALL], ACT.Identity).then_inc(small_ev, 1)
                if ahead and not is_step(i, TILES - 1):
                    normalise(i + 1, 1 - par, i if behind else None)
                if ahead:
                    act.wait_ge(topd_done, i + 1)
                    nc.scalar.activation(top_e[:], top_d[:], ACT.Exp).then_inc(tope_done, 1)
                    act.wait_ge(tsum_done, i + 1)
                    nc.scalar.activation(top_ln[:], top_sum[:], ACT.Ln).then_inc(ln_done, 1)
                    act.wait_ge(corrd_done, i + 1)
                    if behind:
                        act.wait_ge(wlag_done, i)
                    nc.scalar.activation(corr_e[:], corr_d[:], ACT.Exp).then_inc(corre_done, 1)
                if ffn:
                    act.wait_ge(main_mm, i - 2)
                    if not is_step(i, 3):
                        act.wait_ge(base_done, i - 3)
                    nc.scalar.activation(main_g[:], b_main[:], ACT.Copy, scale=gate_t[:, 1:2]).then_inc(main_ev, 1)
                if group is not None and par == 1:
                    gate_exp(group)

            run_steps(act, step)
            gate_exp(GROUPS - 1)

            for g in range(LORA_GROUPS):
                act.wait_ge(st_mm, g + 1)
                nc.scalar.activation(scaled_t[:, g * LORA_GROUP * P:(g + 1) * LORA_GROUP * P], b_st[g][:], ACT.Identity).then_inc(st_ev, 1)

        @block.vector
        def _(dve):
            def stats(i, par, k, free):
                dve.wait_ge(x_in[par], k)
                if free is not None:
                    dve.wait_ge(nmr_done, free)
                held(0)
                nc.vector.bn_stats(bn[:, par, :], at(x_all, i)).then_inc(bn_done, 1)
                dve.wait_ge(bn_done, i + 1)
                held(1)
                nc.vector.bn_aggr(mv[:, par, :], bn[:, par, :]).then_inc(mv_done, 1)

            LINKS = (10, 7)

            def gating(group, half):
                links = [group * sum(LINKS) + LINKS[0] * half, 0]
                if isinstance(group, int):
                    tiles = slice(group * GROUP, (group + 1) * GROUP)
                else:
                    tiles = bass.ds(group * GROUP, GROUP)
                hid = small[:, tiles, ER:SMALL]
                wide = [P, GROUP, G1]
                experts = [P, GROUP, E]

                def link(ins):
                    links[1] += 1
                    ins.then_inc(gchain, 1)
                    dve.wait_ge(gchain, links[0] + links[1])

                def along(v, shape):
                    return v[:].unsqueeze(2).broadcast_to(shape)

                def over(v, shape):
                    return v[:].unsqueeze(1).broadcast_to(shape)

                if half == 0:
                    dve.wait_ge(small_ev, group * GROUP + GROUP)
                    link(nc.vector.tensor_tensor(h[:], hid, over(gb1_b, wide), ALU.add))
                    held(5)
                    for j in range(GROUP):
                        ins = nc.vector.bn_stats(bn_h[:, j, :], h[:, j, :])
                    link(ins)
                    held(6)
                    for j in range(GROUP):
                        ins = nc.vector.bn_aggr(mv_h[:, j, :], bn_h[:, j, :])
                    ins.then_inc(gvar_ready, 1)
                    dve.wait_ge(gvar_ready, group + 1)
                    link(nc.vector.tensor_tensor(h[:], h[:], mv_h[:, :, 0:1].broadcast_to(wide), ALU.subtract))
                    dve.wait_ge(grstd_done, group + 1)
                    link(nc.vector.tensor_tensor(h[:], h[:], along(hr, wide), ALU.mult))
                    link(nc.vector.tensor_tensor(h[:], h[:], over(gamma_b, wide), ALU.mult))
                    link(nc.vector.tensor_tensor(h[:], h[:], over(beta_b, wide), ALU.add))
                    link(nc.vector.tensor_scalar(h[:], h[:], 0.0, None, ALU.max))
                    full = [P, GROUP, E, G1]
                    link(nc.vector.tensor_tensor(gprod[:], h[:].unsqueeze(2).broadcast_to(full),
                                                 gw2_b[:].unsqueeze(1).broadcast_to(full), ALU.mult))
                    link(nc.vector.tensor_reduce(gate[:], gprod[:], AX_X, ALU.add))
                    link(nc.vector.tensor_tensor(gate[:], gate[:], over(gb2_b, experts), ALU.add))
                else:
                    held(7)
                    for j in range(GROUP):
                        ins = nc.vector.max(best[:, j, :], gate[:, j, :])
                    link(ins)
                    held(8)
                    for j in range(GROUP):
                        ins = nc.vector.max_index(best_at[:, j, :], best[:, j, :], gate[:, j, :])
                    link(ins)
                    nc.vector.tensor_tensor(gd[:], best[:, :, 1], best[:, :, 0], ALU.subtract).then_inc(gdiff_ready, 1)
                    both = [P, GROUP, 2, E]
                    link(nc.vector.tensor_tensor(onehot[:, tiles, :, :], best_at[:, :, 0:2].unsqueeze(3).broadcast_to(both),
                                                 index_b[:].unsqueeze(1).unsqueeze(1).broadcast_to(both), ALU.is_equal))
                    dve.wait_ge(gexp_done, group + 1)
                    link(nc.vector.tensor_scalar(gs[:], ge[:], 1.0, None, ALU.add))
                    link(nc.vector.reciprocal(p_top[:, :, 0], gs[:]))
                    link(nc.vector.tensor_tensor(p_top[:, :, 1], ge[:], p_top[:, :, 0], ALU.mult))
                    link(nc.vector.tensor_tensor(weighted[:, tiles, :, :], onehot[:, tiles, :, :],
                                                 p_top[:].unsqueeze(3).broadcast_to(both), ALU.mult))
                assert links[1] == LINKS[half], links

            def step(i, par, ahead, behind, norm, ffn, group):
                if norm:
                    dve.wait_ge(out_mm, i - 1)
                    nc.vector.scalar_tensor_tensor(out=at(x_all, i - 2), in0=b_out[:], scalar=gate_t[:, 0:1], in1=at(x_all, i - 2),
                                                   op0=ALU.mult, op1=ALU.add).then_inc(x1_done, 1)
                    dve.wait_ge(x1_done, i - 1)
                    if not is_step(i, 2) and not is_step(i, 3):
                        dve.wait_ge(nmr2_done, i - 3)
                    held(3)
                    nc.vector.bn_stats(bn2[:, par, :], at(x_all, i - 2)).then_inc(bn2_done, 1)
                    dve.wait_ge(bn2_done, i - 1)
                    held(4)
                    nc.vector.bn_aggr(mv2[:, par, :], bn2[:, par, :]).then_inc(mv2_done, 1)
                if ahead:
                    dve.wait_ge(q_mm, i + 1)
                    dve.wait_ge(even_ev, i + 1)
                    if behind:
                        dve.wait_ge(corr_mm, i)
                    nc.vector.tensor_tensor(prod_q[:, 0, :], b_q[:], v_even[:, par, :], ALU.mult).then_inc(pq_done, 1)
                    nc.vector.tensor_tensor(prod_q[:, 1, :], b_q[:], v_even_sw[:, par, :], ALU.mult).then_inc(pq_done, 1)
                if behind:
                    dve.wait_ge(we_mm, i)
                    dve.wait_ge(even_ev, i)
                    if not is_step(i, 1):
                        dve.wait_ge(out_mm, i - 1)
                    nc.vector.tensor_tensor(prod_w[:, 0, :], b_we[:], v_even[:, 1 - par, :], ALU.mult).then_inc(pe_done, 1)
                    nc.vector.tensor_tensor(prod_w[:, 1, :], b_we[:], v_even_sw[:, 1 - par, :], ALU.mult).then_inc(pe_done, 1)
                    dve.wait_ge(wo_ev, i)
                    dve.wait_ge(odd_ev, i)
                    nc.vector.tensor_tensor(prod_w[:, 2, :], b_wo[:], v_odd[:, 1 - par, :], ALU.mult).then_inc(po_done, 1)
                if ahead and not is_step(i, TILES - 1):
                    stats(i + 1, 1 - par, ((i + 1) // 2 + 1) * 16 if isinstance(i, int) else (i + (2 + par)) * 8,
                          i if behind else None)
                if ahead:
                    dve.wait_ge(corr_mm, i + 1)
                    held(2)
                    corr = b_corr[:].rearrange("p (j l) -> p j l", l=L)
                    for j in range(8):
                        best = nc.vector.max(top[:, j, :], corr[:, j, :])
                    best.then_inc(top_done, 1)
                    dve.wait_ge(top_done, i + 1)
                    if behind:
                        dve.wait_ge(tope_done, i)
                    nc.vector.tensor_tensor(top_d[:], top[:], top[:, :, 0:1].broadcast_to([P, 8, 8]), ALU.subtract).then_inc(topd_done, 1)
                    for j in range(8):
                        repl = nc.vector.match_replace(out=rest[:, j, :], in_to_replace=top[:, j, :], in_values=corr[:, j, :], imm_value=LOW)
                    repl.then_inc(rest_done, 1)
                    dve.wait_ge(tope_done, i + 1)
                    nc.vector.tensor_reduce(top_sum[:], top_e[:], AX_X, ALU.add).then_inc(tsum_done, 1)
                if ahead:
                    dve.wait_ge(ln_done, i + 1)
                    nc.vector.tensor_tensor(shift[:], top[:, :, 0], top_ln[:], ALU.add).then_inc(shift_done, 1)
                    dve.wait_ge(shift_done, i + 1)
                    nc.vector.tensor_tensor(corr_d[:], corr, shift[:].unsqueeze(2).broadcast_to([P, 8, L]), ALU.subtract).then_inc(corrd_done, 1)
                if ahead:
                    dve.wait_ge(rest_done, i + 1)
                    dve.wait_ge(corre_done, i + 1)
                    if behind:
                        dve.wait_ge(turn_mm, i)
                    nc.vector.scalar_tensor_tensor(out=w_lag[:], in0=rest[:], scalar=LOW, in1=corr_e[:],
                                                   op0=ALU.is_equal, op1=ALU.mult).then_inc(wlag_done, 1)
                if group is not None:
                    gating(group, par)

            dve.wait_ge(tanh_done, 1)
            nc.vector.tensor_scalar(gate_r[:], gate_t[:, 1:2], 1.0 / R, None, ALU.mult).then_inc(gate_r_done, 1)
            stats(0, 0, 16, None)
            run_steps(dve, step)
            gating(GROUPS - 1, 1)

            dve.wait_ge(gchain, GROUPS * sum(LINKS))
            nc.vector.tensor_reduce(ohsum[:], onehot[:].rearrange("p n k e -> p k e n"), AX_X, ALU.add).then_inc(ohsum_done, 1)
            dve.wait_ge(count_mm, 1)
            nc.vector.tensor_scalar(allowed[:].rearrange("p k e -> p (k e)"), b_out[:, 0:2 * E], float(CAPACITY), None, ALU.is_le).then_inc(allowed_done, 1)
            dve.wait_ge(allowed_done, 1)
            nc.vector.tensor_tensor(weighted[:], weighted[:], allowed[:].unsqueeze(1).broadcast_to([P, TILES, 2, E]), ALU.mult).then_inc(wexp_chain, 1)
            dve.wait_ge(wexp_chain, 1)
            nc.vector.tensor_tensor(w_exp[:], weighted[:, :, 0, :], weighted[:, :, 1, :], ALU.add).then_inc(wexp_chain, 1)
            dve.wait_ge(wexp_chain, 2)
            dve.wait_ge(gate_r_done, 1)

            full = [P, LORA_GROUP, E, R]
            for g in range(LORA_GROUPS):
                tiles = slice(g * LORA_GROUP, (g + 1) * LORA_GROUP)
                nc.vector.tensor_tensor(scaled[:, g, :, :].rearrange("p n (e r) -> p n e r", r=R),
                                        small[:, tiles, 0:ER].rearrange("p n (e r) -> p n e r", r=R),
                                        w_exp[:, tiles, :].unsqueeze(3).broadcast_to(full), ALU.mult).then_inc(scaled_done, 1)
            for n in range(TILES):
                dve.wait_ge(lora_mm, n + 1)
                nc.vector.scalar_tensor_tensor(out=at(ctx_all, n), in0=b_lora[n % LORA_GROUP][:], scalar=gate_r[:, 0:1],
                                               in1=at(ctx_all, n), op0=ALU.mult, op1=ALU.add).then_inc(result_done, 1)


def kernel(**inputs):
    import concourse.bacc as bacc
    from concourse.bass_utils import run_bass_kernel_spmd as run

    def f(name):
        return np.ascontiguousarray(inputs[name])

    arrays = {
        "x": f("x").reshape(BATCH * L, D),
        "ctx": f("ctx_4096").reshape(BATCH * L, D),
        "mats": transform_matrices(),
        "index": np.arange(E).astype(np.float32),
        "g_xattn": f("g_xattn"),
        "g_ffn": f("g_ffn"),
        "weight_t": np.ascontiguousarray(f("L0_ffn_weight").T),
        "small_t": np.ascontiguousarray(np.concatenate(
            [f("L0_ffn_lora_A").transpose(1, 0, 2).reshape(D, ER), f("L0_ffn_gw1").T], axis=1)),
        "lora_b": f("L0_ffn_lora_B").reshape(ER, D),
        "gb1": f("L0_ffn_gb1"),
        "gamma": f("L0_ffn_ln_gamma"),
        "beta": f("L0_ffn_ln_beta"),
        "gw2": f("L0_ffn_gw2"),
        "gb2": f("L0_ffn_gb2"),
    }
    nc = bacc.Bacc("TRN2", target_bir_lowering=False, num_devices=1)
    aps = [nc.dram_tensor(f"in_{n}", a.shape, F32, kind="ExternalInput").ap() for n, a in arrays.items()]
    out = nc.dram_tensor("out_x", (BATCH * L, D), F32, kind="ExternalOutput").ap()
    build(nc, *aps, out)
    r = run(nc, [{f"in_{n}": a for n, a in arrays.items()}], core_ids=[0])
    return r.results[0]["out_x"].reshape(BATCH, L, D)
```

```python
from contextlib import ExitStack

import numpy as np

import concourse.bass as bass
from concourse import mybir

F32 = mybir.dt.float32
F32R = mybir.dt.float32r
ALU = mybir.AluOpType
ACT = mybir.ActivationFunctionType
AX_X = mybir.AxisListType.X

L = 64
HALF = L // 2
D = 512
P = 128
BATCH = 32
TILES = BATCH * L // P
CHUNKS = D // P
E = 8
R = 16
G1 = 4 * E
ER = E * R
SMALL = ER + G1
COLS = (SMALL + D) // 2
FIRST = COLS - SMALL
PARAMS_AT = 10
CAPACITY = int(3.0 * BATCH * L / E)
LN_EPS = 1e-5
LOW = -3.0e38
GROUP = 2
GROUPS = TILES // GROUP
LORA_GROUP = 4
LORA_GROUPS = TILES // LORA_GROUP
MATRICES = ["ctx_even", "ctx_odd", "fwd_even", "fwd_odd", "corr_same", "corr_swap",
            "out_even_same", "out_even_swap", "out_odd_same", "out_odd_swap", "identity"]
SPLIT = 4


def transform_matrices():
    t = np.arange(L)
    f = np.arange(HALF)
    even = 2 * np.pi * np.outer(t, f) / L
    odd = 2 * np.pi * np.outer(t, 2 * f + 1) / (2 * L)
    sign = (-1.0) ** t

    def forward(real, imag):
        m = np.zeros((2, L, 2, 2, HALF))
        for b in range(2):
            m[b, :, 0, b, :] = real
            m[b, :, 1, b, :] = imag
        return m.reshape(P, P)

    def inverse(part0, part1):
        m = np.zeros((2, 2, HALF, 2, L))
        for b in range(2):
            m[0, b, :, b, :] = part0
            m[1, b, :, b, :] = part1
        return m.reshape(P, P)

    er, ei = np.cos(even), -np.sin(even)
    ei[:, 0] = sign
    ger = er.copy()
    ger[L - 1, 0] = 1.0 + L
    orr, oi = np.cos(odd), -np.sin(odd)
    gor, goi = orr.copy(), oi.copy()
    gor[L - 1] -= orr.sum(0)
    goi[L - 1] -= oi.sum(0)
    ec, es = np.cos(even).T / L, np.sin(even).T / L
    oc, os_ = np.cos(odd).T / L, np.sin(odd).T / L
    c0, c1 = 2 * ec, 2 * ec
    c0[0] = 0.0
    c1 = c1.copy()
    c1[0] = sign / L
    o0, o1 = ec.copy(), ec.copy()
    o0[0] = 0.5 / L
    o1[0] = 0.5 * sign / L
    out = [forward(ger, ei), forward(gor, goi), forward(er, ei), forward(orr, oi),
           inverse(c0, c1), inverse(2 * es, -2 * es),
           inverse(o0, o1), inverse(-es, es),
           inverse(oc, oc), inverse(-os_, os_), np.eye(P)]
    return np.ascontiguousarray(np.concatenate(out, axis=1).astype(np.float32))




def build(nc, x, ctx, mats, index, g_xattn, g_ffn, params_t, lora_b, gb1, gamma, beta, gw2, gb2, out):
    with ExitStack() as stack:
        def sb(name, shape, dtype=F32):
            return stack.enter_context(nc.sbuf_tensor(name, shape, dtype))

        def ps(name):
            return stack.enter_context(nc.psum_tensor(name, [P, 512], F32))

        def sem(name):
            return stack.enter_context(nc.semaphore(name))

        x_all = sb("x_all", [P, TILES, D])
        ctx_all = sb("ctx_all", [P, TILES, D])
        mat = sb("mat", [P, len(MATRICES), P])
        xn = sb("xn", [P, 2, D])
        v_even = sb("v_even", [P, 2, D])
        v_even_sw = sb("v_even_sw", [P, 2, D])
        v_odd = sb("v_odd", [P, 2, D])
        v_odd_sw = sb("v_odd_sw", [P, 2, D])
        prod_q = sb("prod_q", [P, 2, D])
        prod_w = sb("prod_w", [P, 4, D])
        top = sb("top", [P, 8, 8])
        rest = sb("rest", [P, 8, L])
        top_d = sb("top_d", [P, 8, 8])
        top_e = sb("top_e", [P, 8, 8])
        top_sum = sb("top_sum", [P, 8])
        top_ln = sb("top_ln", [P, 8])
        neg_shift = sb("neg_shift", [P, 8])
        corr_e = sb("corr_e", [P, 8, L])
        w_lag = sb("w_lag", [P, 8, L])
        w_hi, w_lo = sb("w_hi", [P, D], F32R), sb("w_lo", [P, D], F32R)
        ctx_hi, ctx_lo = sb("ctx_hi", [P, 2, D], F32R), sb("ctx_lo", [P, 2, D], F32R)
        mat_hi, mat_lo = sb("mat_hi", [P, SPLIT, P], F32R), sb("mat_lo", [P, SPLIT, P], F32R)
        x_hi, x_lo = sb("x_hi", [P, D], F32R), sb("x_lo", [P, D], F32R)
        param_hi, param_lo = sb("param_hi", [P, CHUNKS, SMALL + D], F32R), sb("param_lo", [P, CHUNKS, SMALL + D], F32R)
        lora_hi, lora_lo = sb("lora_hi", [P, D], F32R), sb("lora_lo", [P, D], F32R)
        xn_hi, xn_lo = sb("xn_hi", [P, 2, D], F32R), sb("xn_lo", [P, 2, D], F32R)
        bn = sb("bn", [P, 2, 6])
        mv = sb("mv", [P, 2, 2])
        var_eps = sb("var_eps", [P, 2])
        rstd = sb("rstd", [P, 2])
        nmr = sb("nmr", [P, 2])
        scratch = sb("scratch", [P, 12])
        pool_scratch = sb("pool_scratch", [P, 5])
        eps_c = sb("eps_c", [P, GROUP])
        neg_c = sb("neg_c", [P, GROUP])
        m_half = sb("m_half", [P, GROUP])
        bn_x1 = sb("bn_x1", [P, 2, 6])
        mv_x1 = sb("mv_x1", [P, 2, 2])
        var_eps_x1 = sb("var_eps_x1", [P, 2])
        rstd_x1 = sb("rstd_x1", [P, 2])
        nmr_x1 = sb("nmr_x1", [P, 2])
        gates_raw = sb("gates_raw", [P, 2])
        gate_t = sb("gate_t", [P, 2])
        gate_r = sb("gate_r", [P, 1])
        params = x_all[:, PARAMS_AT:, :].rearrange("p n d -> p (n d)")[:, 0:CHUNKS * (SMALL + D)].rearrange("p (c n) -> p c n", c=CHUNKS)
        w_b = sb("w_b", [P, D])
        gb1_b = sb("gb1_b", [P, G1])
        gamma_b = sb("gamma_b", [P, G1])
        beta_b = sb("beta_b", [P, G1])
        gw2_b = sb("gw2_b", [P, E, G1])
        gb2_b = sb("gb2_b", [P, E])
        index_b = sb("index_b", [P, E])
        x1n = sb("x1n", [P, D])
        wo_sb = sb("wo_sb", [P, D])
        main_g = sb("main_g", [P, D])
        small = sb("small", [P, TILES, SMALL])
        h = sb("h", [P, GROUP, G1])
        bn_h = sb("bn_h", [P, GROUP, 6])
        mv_h = sb("mv_h", [P, GROUP, 2])
        var_eps_h = sb("var_eps_h", [P, GROUP])
        rstd_h = sb("rstd_h", [P, GROUP])
        gprod = sb("gprod", [P, GROUP, E, G1])
        gate = sb("gate", [P, GROUP, E])
        best = sb("best", [P, GROUP, E])
        best_at = stack.enter_context(nc.sbuf_tensor("best_at", [P, GROUP, E], mybir.dt.uint32))
        gate_diff = sb("gate_diff", [P, GROUP])
        gate_exp_diff = sb("gate_exp_diff", [P, GROUP])
        gate_exp_sum = sb("gate_exp_sum", [P, GROUP])
        p_top = sb("p_top", [P, GROUP, 2])
        onehot = sb("onehot", [P, TILES, 2, E])
        weighted = sb("weighted", [P, TILES, 2, E])
        ohsum = sb("ohsum", [P, 2, E])
        ones = sb("ones", [P, P])
        allowed = sb("allowed", [P, 2, E])
        w_exp = sb("w_exp", [P, TILES, E])
        scaled = x_all[:, 0:LORA_GROUPS, :].rearrange("p g (j c) -> p g j c", c=ER)
        scaled_hi, scaled_lo = sb("scaled_hi", [P, TILES * P], F32R), sb("scaled_lo", [P, TILES * P], F32R)

        b_even, b_odd, b_q, b_corr, b_turn, b_we, b_wo, b_out = [
            ps(n) for n in ("b_even", "b_odd", "b_q", "b_corr", "b_turn", "b_we", "b_wo", "b_out")]
        b_small = b_even
        b_xt = b_out
        b_main = b_turn
        b_scaled = [b_wo, b_we, b_turn, b_corr]
        b_lora = [b_even, b_odd, b_q, b_out]

        x_in = [sem("x_in0"), sem("x_in1")]
        ctx_in = [sem("ctx_in0"), sem("ctx_in1")]
        mats_split_in, mats_in, gates_in, params_in = sem("mats_split_in"), sem("mats_in"), sem("gates_in"), sem("params_in")
        consts_set = sem("consts_set")
        tanh_done, gate_r_done = sem("tanh_done"), sem("gate_r_done")
        bn_done, mv_done, var_done, rstd_done, nmr_done, xn_done = [
            sem(n) for n in ("bn_done", "mv_done", "var_done", "rstd_done", "nmr_done", "xn_done")]
        even_mm, odd_mm, q_mm, corr_mm, turn_mm, we_mm, wo_mm, out_mm = [
            sem(n) for n in ("even_mm", "odd_mm", "q_mm", "corr_mm", "turn_mm", "we_mm", "wo_mm", "out_mm")]
        even_ev, odd_ev = sem("even_ev"), sem("odd_ev")
        prod_q_done, prod_even_done, prod_odd_done = sem("prod_q_done"), sem("prod_even_done"), sem("prod_odd_done")
        top_done, rest_done, topd_done, tope_done, tsum_done, ln_done, shift_done, corre_done, wlag_done = [
            sem(n) for n in ("top_done", "rest_done", "topd_done", "tope_done", "tsum_done", "ln_done",
                             "shift_done", "corre_done", "wlag_done")]
        wo_ev, prod_odd_sw_done, main_ev, pool_held = sem("wo_ev"), sem("prod_odd_sw_done"), sem("main_ev"), sem("pool_held")
        mat_hi_done, mat_lo_done, ctx_hi_done, ctx_lo_done, w_hi_done, w_lo_done, x_hi_done, x_lo_done, param_hi_done, param_lo_done, xn_hi_done, xn_lo_done, scaled_lo_done = [
            sem(n) for n in ("mat_hi_done", "mat_lo_done", "ctx_hi_done", "ctx_lo_done", "w_hi_done", "w_lo_done",
                             "x_hi_done", "x_lo_done", "param_hi_done", "param_lo_done",
                             "xn_hi_done", "xn_lo_done", "scaled_lo_done")]
        mr_done, bn_h_done, relu_done, scaled_pool_done = [sem(n) for n in ("mr_done", "bn_h_done", "relu_done", "scaled_pool_done")]
        x1_done, bn_x1_done, mv_x1_done, var_x1_done, rstd_x1_done, mr_x1_done, nmr_x1_done = [
            sem(n) for n in ("x1_done", "bn_x1_done", "mv_x1_done", "var_x1_done", "rstd_x1_done", "mr_x1_done", "nmr_x1_done")]
        x1n_done, xt_mm, small_mm, small_ev, main_mm, base_done = [
            sem(n) for n in ("x1n_done", "xt_mm", "small_mm", "small_ev", "main_mm", "base_done")]
        hidden_done, gvar_ready, gprod_done, gate_sum_done, choose_chain, gdiff_ready, gexp_done, gate_norm_chain, weigh_chain = [
            sem(n) for n in ("hidden_done", "gvar_ready", "gprod_done", "gate_sum_done", "choose_chain", "gdiff_ready",
                             "gexp_done", "gate_norm_chain", "weigh_chain")]
        ohsum_done, count_mm, allowed_done, wexp_chain, scaled_done, scaled_turned, scaled_hi_done, lora_mm, result_done = [
            sem(n) for n in ("ohsum_done", "count_mm", "allowed_done", "wexp_chain", "scaled_done",
                             "scaled_turned", "scaled_hi_done", "lora_mm", "result_done")]
        stored = [sem("stored0"), sem("stored1")]

        def m(name):
            return mat[:, MATRICES.index(name), :]

        def split_product(bank, a_hi, a_lo, b_hi, b_lo, b_lo_ready=None):
            nc.tensor.matmul(bank[:], a_hi, b_hi, start=True, stop=False)
            nc.tensor.matmul(bank[:], a_lo, b_hi, start=False, stop=False)
            if b_lo_ready is not None:
                nc.tensor.wait_ge(*b_lo_ready)
            return nc.tensor.matmul(bank[:], a_hi, b_lo, start=False, stop=True)

        def m_parts(name):
            k = MATRICES.index(name)
            return mat_hi[:, k, :], mat_lo[:, k, :]

        def at(buf, i):
            if isinstance(i, int):
                return buf[:, i, :]
            return buf[:, bass.ds(i, 1), :].rearrange("p a d -> p (a d)")

        x_rows = x.rearrange("(n p) d -> n p d", p=P)
        ctx_rows = ctx.rearrange("(n p) d -> n p d", p=P)
        out_rows = out.rearrange("(n p) d -> n p d", p=P)

        def row(src, i):
            if isinstance(i, int):
                return src[i, :, :]
            return src[bass.ds(i, 1), :, :].rearrange("a p d -> (a p) d")

        def scale(engine, g):
            tiles = slice(g * LORA_GROUP, (g + 1) * LORA_GROUP)
            return engine.tensor_tensor(scaled[:, g, :, :].rearrange("p n (e r) -> p n e r", r=R),
                                        small[:, tiles, 0:ER].rearrange("p n (e r) -> p n e r", r=R),
                                        w_exp[:, tiles, :].unsqueeze(3).broadcast_to([P, LORA_GROUP, E, R]), ALU.mult)

        def held(use):
            nc.vector.memset(scratch[:, use:use + 1], 0.0)

        def run_steps(eng, step):
            step(0, 0, True, False, False, False, None)
            step(1, 1, True, True, False, False, None)
            step(2, 0, True, True, True, False, None)
            step(3, 1, True, True, True, True, None)
            step(4, 0, True, True, True, True, None)
            with eng.Fori(1, TILES // 2 - 2) as r:
                step(r * 2 + 3, 1, True, True, True, True, r - 1)
                step(r * 2 + 4, 0, True, True, True, True, r - 1)
            step(TILES - 1, 1, True, True, True, True, GROUPS - 3)
            step(TILES, 0, False, True, True, True, GROUPS - 3)
            step(TILES + 1, 1, False, False, True, True, GROUPS - 2)
            step(TILES + 2, 0, False, False, False, True, GROUPS - 2)

        def is_step(i, n):
            return isinstance(i, int) and i == n

        block = stack.enter_context(nc.Block())

        @block.sync
        def _(sp):
            def load(i, par, again):
                if again is not None:
                    sp.wait_ge(x_in[par], i // 2 * 16 if isinstance(i, int) else again * 16)
                    sp.wait_ge(ctx_in[par], i // 2 * 16 if isinstance(i, int) else again * 16)
                sp.dma_start(at(x_all, i), row(x_rows, i)).then_inc(x_in[par], 16)
                sp.dma_start(at(ctx_all, i), row(ctx_rows, i)).then_inc(ctx_in[par], 16)

            sp.dma_start(at(x_all, 0), x_rows[0, :, :]).then_inc(x_in[0], 16)
            sp.dma_start(mat[:, 0:SPLIT, :], mats.rearrange("p (n m) -> p n m", m=P)[:, 0:SPLIT, :]).then_inc(mats_split_in, 16)
            sp.dma_start(at(ctx_all, 0), ctx_rows[0, :, :]).then_inc(ctx_in[0], 16)
            sp.dma_start(gates_raw[:, 0:1], g_xattn.rearrange("(a n) -> a n", a=1).broadcast_to([P, 1])).then_inc(gates_in, 16)
            sp.dma_start(gates_raw[:, 1:2], g_ffn.rearrange("(a n) -> a n", a=1).broadcast_to([P, 1])).then_inc(gates_in, 16)
            sp.dma_start(mat[:, SPLIT:, :], mats.rearrange("p (n m) -> p n m", m=P)[:, SPLIT:, :]).then_inc(mats_in, 16)
            load(1, 1, None)
            load(2, 0, 1)
            load(3, 1, 1)
            sp.dma_start(params, params_t.rearrange("(c p) n -> p c n", p=P)).then_inc(params_in, 16)
            sp.dma_start(w_b[:], lora_b).then_inc(params_in, 16)
            for dst, src, n in ((gb1_b, gb1, G1), (gamma_b, gamma, G1), (beta_b, beta, G1), (gb2_b, gb2, E), (index_b, index, E)):
                sp.dma_start(dst[:], src.rearrange("(a n) -> a n", a=1).broadcast_to([P, n])).then_inc(params_in, 16)
            sp.dma_start(gw2_b[:].rearrange("p e g -> p (e g)"),
                         gw2.rearrange("(a e) g -> a (e g)", a=1).broadcast_to([P, E * G1])).then_inc(params_in, 16)
            with sp.Fori(2, PARAMS_AT // 2) as r:
                load(r * 2, 0, r)
                load(r * 2 + 1, 1, r)
            sp.wait_ge(param_lo_done, 2)
            with sp.Fori(PARAMS_AT // 2, TILES // 2) as r:
                load(r * 2, 0, r)
                load(r * 2 + 1, 1, r)

            for n in range(TILES):
                sp.wait_ge(result_done, n + 1)
                sp.dma_start(out_rows[n, :, :], ctx_all[:, n, :]).then_inc(stored[n % 2], 16)
            sp.wait_ge(stored[0], 16 * (TILES // 2))
            sp.wait_ge(stored[1], 16 * (TILES // 2))

        PARAMS = 16 * 8
        LINKS = 4
        GATE_LINKS = 6

        @block.gpsimd
        def _(pool):
            nc.gpsimd.memset(m_half[:], -0.5).then_inc(consts_set, 1)
            nc.gpsimd.memset(ones[:], 1.0).then_inc(consts_set, 1)
            nc.gpsimd.memset(eps_c[:], LN_EPS).then_inc(consts_set, 1)
            nc.gpsimd.memset(neg_c[:], -1.0).then_inc(consts_set, 1)
            nc.gpsimd.memset(gate_exp_sum[:], 0.0).then_inc(weigh_chain, 1)
            pool.wait_ge(consts_set, 4)

            def pool_hold(use):
                nc.gpsimd.tensor_tensor(pool_scratch[:, use:use + 1], eps_c[:, 0:1], neg_c[:, 0:1], ALU.mult).then_inc(pool_held, 1)

            def powers(stat, k, par, var_, rs_, nm_, ready, sems):
                var_s, rs_s, mr_s, nm_s = sems
                col = slice(par, par + 1)
                pool.wait_ge(ready, k)
                nc.gpsimd.tensor_tensor(var_[:, col], stat[:, par, 1:2], eps_c[:, 0:1], ALU.add).then_inc(var_s, 1)
                pool.wait_ge(var_s, k)
                nc.gpsimd.tensor_tensor(rs_[:, col], var_[:, col], m_half[:, 0:1], ALU.pow).then_inc(rs_s, 1)
                pool.wait_ge(rs_s, k)
                nc.gpsimd.tensor_tensor(nm_[:, col], stat[:, par, 0:1], rs_[:, col], ALU.mult).then_inc(mr_s, 1)
                pool.wait_ge(mr_s, k)
                nc.gpsimd.tensor_tensor(nm_[:, col], nm_[:, col], neg_c[:, 0:1], ALU.mult).then_inc(nm_s, 1)

            wide = [P, GROUP, G1]

            def gate_hidden(group):
                tiles = slice(group * GROUP, (group + 1) * GROUP) if isinstance(group, int) else bass.ds(group * GROUP, GROUP)
                pool.wait_ge(small_ev, group * GROUP + GROUP)
                pool_hold(2)
                nc.gpsimd.tensor_tensor(h[:], small[:, tiles, ER:SMALL], gb1_b[:].unsqueeze(1).broadcast_to(wide), ALU.add).then_inc(hidden_done, 1)

            def gate_norm(group):
                def along(v):
                    return v.broadcast_to(wide)

                def over(v):
                    return v[:].unsqueeze(1).broadcast_to(wide)

                def link(k, ins):
                    ins.then_inc(gate_norm_chain, 1)
                    pool.wait_ge(gate_norm_chain, group * GATE_LINKS + k)

                pool.wait_ge(gvar_ready, group + 1)
                link(1, nc.gpsimd.tensor_tensor(var_eps_h[:], mv_h[:, :, 1], eps_c[:], ALU.add))
                nc.gpsimd.tensor_tensor(rstd_h[:], var_eps_h[:], m_half[:], ALU.pow)
                link(2, nc.gpsimd.tensor_tensor(h[:], h[:], along(mv_h[:, :, 0:1]), ALU.subtract))
                link(3, nc.gpsimd.tensor_tensor(h[:], h[:], along(rstd_h[:].unsqueeze(2)), ALU.mult))
                link(4, nc.gpsimd.tensor_tensor(h[:], h[:], over(gamma_b), ALU.mult))
                link(5, nc.gpsimd.tensor_tensor(h[:], h[:], over(beta_b), ALU.add))
                if isinstance(group, int) and group == GROUPS - 1:
                    return
                pool_hold(3)
                link(6, nc.gpsimd.tensor_scalar(h[:], h[:], 0.0, None, ALU.max))
                pool.wait_ge(gate_sum_done, group + 1)
                full = [P, GROUP, E, G1]
                nc.gpsimd.tensor_tensor(gprod[:], h[:].unsqueeze(2).broadcast_to(full),
                                        gw2_b[:].unsqueeze(1).broadcast_to(full), ALU.mult).then_inc(gprod_done, 1)

            def weigh(group):
                both = [P, GROUP, 2, E]
                tiles = slice(group * GROUP, (group + 1) * GROUP) if isinstance(group, int) else bass.ds(group * GROUP, GROUP)

                def link(k, ins):
                    ins.then_inc(weigh_chain, 1)
                    pool.wait_ge(weigh_chain, group * LINKS + (k + 1))

                pool.wait_ge(gexp_done, group + 1)
                link(1, nc.gpsimd.tensor_tensor(gate_exp_sum[:], gate_exp_diff[:], ones[:, 0:GROUP], ALU.add))
                link(2, nc.gpsimd.tensor_tensor(p_top[:, :, 0], gate_exp_sum[:], neg_c[:], ALU.pow))
                link(3, nc.gpsimd.tensor_tensor(p_top[:, :, 1], gate_exp_diff[:], p_top[:, :, 0], ALU.mult))
                pool.wait_ge(choose_chain, group * LINKS + LINKS)
                pool_hold(4)
                link(4, nc.gpsimd.tensor_tensor(weighted[:, tiles, :, :], onehot[:, tiles, :, :],
                                                p_top[:].unsqueeze(3).broadcast_to(both), ALU.mult))

            def ctx_split(i, par):
                pool.wait_ge(ctx_hi_done, i + 1)
                if not (isinstance(i, int) and i < 2):
                    pool.wait_ge(odd_mm, i - 1)
                pool_hold(0)
                nc.gpsimd.tensor_tensor(ctx_lo[:, par, :], at(ctx_all, i), ctx_hi[:, par, :], ALU.subtract).then_inc(ctx_lo_done, 1)

            def xn_split(i, par):
                pool.wait_ge(xn_hi_done, i + 1)
                if not (isinstance(i, int) and i < 2):
                    pool.wait_ge(q_mm, i - 1)
                nc.gpsimd.tensor_tensor(xn_lo[:, par, :], xn[:, par, :], xn_hi[:, par, :], ALU.subtract).then_inc(xn_lo_done, 1)

            def base(n):
                pool.wait_ge(main_ev, n + 1)
                pool_hold(1)
                nc.gpsimd.tensor_tensor(at(ctx_all, n), main_g[:], at(x_all, n), ALU.add).then_inc(base_done, 1)

            def powers_x1(i, par):
                if not is_step(i, 2) and not is_step(i, 3):
                    pool.wait_ge(x1n_done, i - 3)
                powers(mv_x1, i - 1, par, var_eps_x1, rstd_x1, nmr_x1, mv_x1_done, (var_x1_done, rstd_x1_done, mr_x1_done, nmr_x1_done))

            def params_low(k):
                half = slice(k * CHUNKS // 2, (k + 1) * CHUNKS // 2)
                pool.wait_ge(param_hi_done, k + 1)
                nc.gpsimd.tensor_tensor(param_lo[:, half, :], params[:, half, :], param_hi[:, half, :], ALU.subtract).then_inc(param_lo_done, 1)

            def step(i, par, ahead, behind, norm, ffn, group):
                if is_step(i, 2):
                    params_low(1)
                if is_step(i, 0):
                    powers(mv, 1, 0, var_eps, rstd, nmr, mv_done, (var_done, rstd_done, mr_done, nmr_done))
                    ctx_split(0, 0)
                    xn_split(0, 0)
                if ahead and not is_step(i, TILES - 1):
                    if behind:
                        pool.wait_ge(xn_done, i)
                    powers(mv, i + 2, 1 - par, var_eps, rstd, nmr, mv_done, (var_done, rstd_done, mr_done, nmr_done))
                if behind:
                    pool.wait_ge(wo_ev, i)
                    pool.wait_ge(odd_ev, i * 2)
                    if not is_step(i, 1):
                        pool.wait_ge(out_mm, i - 1)
                    nc.gpsimd.tensor_tensor(prod_w[:, 3, :], wo_sb[:], v_odd_sw[:, 1 - par, :], ALU.mult).then_inc(prod_odd_sw_done, 1)
                if ahead and not is_step(i, TILES - 1):
                    ctx_split(i + 1, 1 - par)
                    xn_split(i + 1, 1 - par)
                if is_step(i, 1):
                    params_low(0)
                if is_step(i, 3):
                    pool.wait_ge(param_hi_done, 3)
                    nc.gpsimd.tensor_tensor(lora_lo[:], w_b[:], lora_hi[:], ALU.subtract).then_inc(param_lo_done, 1)
                if norm and not behind:
                    powers_x1(i, par)
                    base(i - 4)
                if group is not None and par == 1:
                    gate_hidden(group)
                if norm and behind:
                    powers_x1(i, par)
                if group is not None and par == 1:
                    gate_norm(group)
                if ffn and not is_step(i, TILES) and not is_step(i, TILES + 2):
                    base(i - 3)
                if group is not None and par == 0 and not is_step(i, TILES + 2):
                    weigh(group)

            run_steps(pool, step)
            gate_hidden(GROUPS - 1)
            gate_norm(GROUPS - 1)
            weigh(GROUPS - 2)
            weigh(GROUPS - 1)
            base(TILES - 1)
            pool.wait_ge(wexp_chain, 2)
            for g in range(LORA_GROUPS // 2, LORA_GROUPS):
                scale(nc.gpsimd, g).then_inc(scaled_pool_done, 1)

        @block.tensor
        def _(pe):
            def token_product(bank, cols):
                for c in range(CHUNKS):
                    tokens = x_hi[:, c * P:(c + 1) * P]
                    pe.matmul(bank[:, 0:COLS], tokens, param_hi[:, c, cols], start=(c == 0), stop=False)
                    pe.matmul(bank[:, 0:COLS], tokens, param_lo[:, c, cols], start=False, stop=False)
                for c in range(CHUNKS):
                    mm = pe.matmul(bank[:, 0:COLS], x_lo[:, c * P:(c + 1) * P], param_hi[:, c, cols], start=False, stop=(c == CHUNKS - 1))
                return mm

            def turned_weights(i, behind, ffn):
                if behind:
                    pe.wait_ge(wlag_done, i)
                    if ffn and not is_step(i, 3):
                        pe.wait_ge(main_ev, i - 3)
                    for c in range(CHUNKS):
                        turn = pe.transpose(b_turn[:, c * P:(c + 1) * P],
                                            w_lag[:].rearrange("p j l -> p (j l)")[:, c * P:(c + 1) * P], m("identity"))
                    turn.then_inc(turn_mm, 1)

            def q_and_odd(i, par, ahead, behind):
                if ahead:
                    pe.wait_ge(xn_lo_done, i + 1)
                    if behind:
                        pe.wait_ge(prod_q_done, i * 2)
                    split_product(b_q, *m_parts("fwd_even"), xn_hi[:, par, :], xn_lo[:, par, :]).then_inc(q_mm, 1)
                if ahead:
                    if behind:
                        pe.wait_ge(odd_ev, i * 2)
                    split_product(b_odd, *m_parts("ctx_odd"), ctx_hi[:, par, :], ctx_lo[:, par, :]).then_inc(odd_mm, 1)

            def second_half(i, behind, ffn):
                if ffn:
                    if not behind:
                        pe.wait_ge(main_ev, i - 3)
                    token_product(b_main, slice(COLS, 2 * COLS)).then_inc(main_mm, 1)

            def attention_out(i, behind):
                if behind:
                    pe.wait_ge(prod_even_done, i * 2)
                    if not is_step(i, 1):
                        pe.wait_ge(x1_done, i - 1)
                    pe.matmul(b_out[:], m("out_even_same"), prod_w[:, 0, :], start=True, stop=False)
                    pe.matmul(b_out[:], m("out_even_swap"), prod_w[:, 1, :], start=False, stop=False)
                    pe.wait_ge(prod_odd_done, i)
                    pe.wait_ge(prod_odd_sw_done, i)
                    pe.matmul(b_out[:], m("out_odd_same"), prod_w[:, 2, :], start=False, stop=False)
                    pe.matmul(b_out[:], m("out_odd_swap"), prod_w[:, 3, :], start=False, stop=True).then_inc(out_mm, 1)

            def step(i, par, ahead, behind, norm, ffn, group):
                if ahead:
                    pe.wait_ge(ctx_hi_done, i + 1)
                    if not behind:
                        pe.wait_ge(mats_in, 16)
                        pe.wait_ge(mat_hi_done, 1)
                        pe.wait_ge(mat_lo_done, 1)
                    else:
                        pe.wait_ge(even_ev, i * 2)
                    if ffn and not is_step(i, 3):
                        pe.wait_ge(small_ev, i - 3)
                    split_product(b_even, *m_parts("ctx_even"), ctx_hi[:, par, :], ctx_lo[:, par, :], (ctx_lo_done, i + 1)).then_inc(even_mm, 1)
                if ffn:
                    turned_weights(i, behind, ffn)
                    q_and_odd(i, par, ahead, behind)
                else:
                    q_and_odd(i, par, ahead, behind)
                    turned_weights(i, behind, ffn)
                if ffn:
                    pe.wait_ge(x1n_done, i - 2)
                    if norm:
                        pe.wait_ge(x1_done, i - 1)
                    else:
                        pe.wait_ge(x_lo_done, i - 3)
                    for c in range(CHUNKS):
                        turn = pe.transpose(b_xt[:, c * P:(c + 1) * P], x1n[:, c * P:(c + 1) * P], m("identity"))
                    turn.then_inc(xt_mm, 1)
                if behind:
                    pe.wait_ge(w_hi_done, i)
                    if not is_step(i, 1):
                        pe.wait_ge(prod_even_done, i * 2 - 2)
                    split_product(b_we, *m_parts("fwd_even"), w_hi[:], w_lo[:], (w_lo_done, i)).then_inc(we_mm, 1)
                    if not is_step(i, 1):
                        pe.wait_ge(prod_odd_done, i - 1)
                        pe.wait_ge(wo_ev, i - 1)
                    split_product(b_wo, *m_parts("fwd_odd"), w_hi[:], w_lo[:]).then_inc(wo_mm, 1)
                if ahead:
                    pe.wait_ge(prod_q_done, i * 2 + 2)
                    for c in range(CHUNKS):
                        pe.matmul(b_corr[:, c * P:(c + 1) * P], prod_q[:, 0, c * P:(c + 1) * P], m("corr_same"), start=True, stop=False)
                        corr = pe.matmul(b_corr[:, c * P:(c + 1) * P], prod_q[:, 1, c * P:(c + 1) * P], m("corr_swap"), start=False, stop=True)
                    corr.then_inc(corr_mm, 1)
                if ffn:
                    if is_step(i, 3):
                        pe.wait_ge(param_lo_done, 2)
                    if ahead:
                        pe.wait_ge(even_ev, i * 2 + 2)
                    elif not is_step(i, TILES):
                        pe.wait_ge(small_ev, i - 3)
                    pe.wait_ge(x_hi_done, i - 2)
                    pe.wait_ge(x_lo_done, i - 2)
                    token_product(b_small, slice(0, COLS)).then_inc(small_mm, 1)
                if ahead:
                    second_half(i, behind, ffn)
                    attention_out(i, behind)
                else:
                    attention_out(i, behind)
                    second_half(i, behind, ffn)

            run_steps(pe, step)

            pe.wait_ge(param_lo_done, 3)
            pe.wait_ge(ohsum_done, 1)
            pe.matmul(b_out[:, 0:2 * E], ones[:], ohsum[:].rearrange("p k e -> p (k e)"), start=True, stop=True).then_inc(count_mm, 1)

            def turn_scaled(g):
                on_pool = g - LORA_GROUPS // 2
                pe.wait_ge(*((scaled_done, g + 1) if on_pool < 0 else (scaled_pool_done, on_pool + 1)))
                if b_scaled[g] is b_main:
                    pe.wait_ge(main_ev, TILES)
                for j in range(LORA_GROUP):
                    turn = pe.transpose(b_scaled[g][:, j * P:(j + 1) * P], scaled[:, g, j, :], m("identity"))
                turn.then_inc(scaled_turned, 1)

            turn_scaled(0)
            turn_scaled(1)
            for n in range(TILES):
                if n % LORA_GROUP == 0:
                    pe.wait_ge(scaled_lo_done, n // LORA_GROUP + 1)
                if n >= LORA_GROUP:
                    pe.wait_ge(result_done, n - LORA_GROUP + 1)
                tokens = slice(n * P, (n + 1) * P)
                bank = b_lora[n % LORA_GROUP]
                pe.matmul(bank[:], scaled_hi[:, tokens], lora_hi[:], start=True, stop=False)
                pe.matmul(bank[:], scaled_hi[:, tokens], lora_lo[:], start=False, stop=False)
                pe.matmul(bank[:], scaled_lo[:, tokens], lora_hi[:], start=False, stop=True).then_inc(lora_mm, 1)
                if n % LORA_GROUP == 2 and n // LORA_GROUP + 2 < LORA_GROUPS:
                    turn_scaled(n // LORA_GROUP + 2)

        @block.scalar
        def _(act):

            def swapped(dst_sw, bank, par, done):
                nc.scalar.activation(dst_sw[0:L, par, :], bank[L:P, :], ACT.Identity)
                nc.scalar.activation(dst_sw[L:P, par, :], bank[0:L, :], ACT.Identity).then_inc(done, 1)

            def spectrum(dst, bank, par, ready, done, i, free):
                act.wait_ge(ready, i + 1)
                for reader, count in free:
                    act.wait_ge(reader, count)
                nc.scalar.activation(dst[:, par, :], bank[:], ACT.Identity).then_inc(done, 1)

            def normalise(i, par, free):
                act.wait_ge(nmr_done, i + 1)
                if free is not None:
                    act.wait_ge(q_mm, free)
                nc.scalar.activation(xn[:, par, :], at(x_all, i), ACT.Identity, bias=nmr[:, par:par + 1],
                                     scale=rstd[:, par:par + 1]).then_inc(xn_done, 1)
                act.wait_ge(xn_done, i + 1)
                nc.scalar.activation(xn_hi[:, par, :], xn[:, par, :], ACT.Identity).then_inc(xn_hi_done, 1)

            def normalise_x1(n, par, k, first):
                act.wait_ge(nmr_x1_done, k)
                if not first:
                    act.wait_ge(xt_mm, k - 1)
                nc.scalar.activation(x1n[:], at(x_all, n), ACT.Identity, bias=nmr_x1[:, par:par + 1],
                                     scale=rstd_x1[:, par:par + 1]).then_inc(x1n_done, 1)

            def gate_exp(group):
                act.wait_ge(gdiff_ready, group + 1)
                act.wait_ge(weigh_chain, group * LINKS + 1)
                nc.scalar.activation(gate_exp_diff[:], gate_diff[:], ACT.Exp).then_inc(gexp_done, 1)

            def ctx_round(i, par):
                act.wait_ge(ctx_in[par], (i // 2 + 1) * 16 if isinstance(i, int) else (i + (2 - par)) * 8)
                if not (isinstance(i, int) and i < 2):
                    act.wait_ge(odd_mm, i - 1)
                nc.scalar.activation(ctx_hi[:, par, :], at(ctx_all, i), ACT.Identity).then_inc(ctx_hi_done, 1)

            act.wait_ge(mats_split_in, 16)
            nc.scalar.activation(mat_hi[:], mat[:, 0:SPLIT, :], ACT.Identity).then_inc(mat_hi_done, 1)
            ctx_round(0, 0)
            act.wait_ge(gates_in, 32)
            nc.scalar.activation(gate_t[:], gates_raw[:], ACT.Tanh).then_inc(tanh_done, 1)
            nc.scalar.preload_act_table_set("natural_log_exp_and_others")

            def weights_high(i, behind):
                if behind:
                    act.wait_ge(turn_mm, i)
                    if not is_step(i, 1):
                        act.wait_ge(wo_mm, i - 1)
                    nc.scalar.activation(w_hi[:], b_turn[:], ACT.Identity).then_inc(w_hi_done, 1)

            def step(i, par, ahead, behind, norm, ffn, group):
                early = isinstance(i, int) and i < 2
                if is_step(i, 0):
                    normalise(0, 0, None)
                if ffn and (ahead or is_step(i, TILES)):
                    normalise_x1(i - 3, 1 - par, i - 2, is_step(i, 3))
                if ahead:
                    spectrum(v_even, b_even, par, even_mm, even_ev, i, () if early else ((prod_even_done, i * 2 - 2),))
                if ffn:
                    weights_high(i, behind)
                if ahead:
                    swapped(v_even_sw, b_even, par, even_ev)
                if not ffn:
                    weights_high(i, behind)
                if ffn:
                    act.wait_ge(xt_mm, i - 2)
                    if not is_step(i, 3):
                        act.wait_ge(main_mm, i - 3)
                    nc.scalar.activation(x_hi[:], b_xt[:], ACT.Identity).then_inc(x_hi_done, 1)
                if behind:
                    act.wait_ge(wo_mm, i)
                    if not is_step(i, 1):
                        act.wait_ge(prod_odd_sw_done, i - 1)
                    nc.scalar.activation(wo_sb[:], b_wo[:], ACT.Identity).then_inc(wo_ev, 1)
                if ahead:
                    spectrum(v_odd, b_odd, par, odd_mm, odd_ev, i, () if early else ((prod_odd_done, i - 1), (prod_odd_sw_done, i - 1)))
                    swapped(v_odd_sw, b_odd, par, odd_ev)
                if ahead and not is_step(i, TILES - 1):
                    ctx_round(i + 1, 1 - par)
                if ahead and not is_step(i, TILES - 1):
                    normalise(i + 1, 1 - par, i if behind else None)
                if ffn:
                    act.wait_ge(small_mm, i - 2)
                    if not is_step(i, 3):
                        act.wait_ge(base_done, i - 3)
                    nc.scalar.activation(at(small, i - 3), b_small[:, 0:SMALL], ACT.Identity)
                    nc.scalar.activation(main_g[:, 0:FIRST], b_small[:, SMALL:COLS], ACT.Copy, scale=gate_t[:, 1:2]).then_inc(small_ev, 1)
                if ahead:
                    act.wait_ge(topd_done, i + 1)
                    nc.scalar.activation(top_e[:], top_d[:], ACT.Exp).then_inc(tope_done, 1)
                    act.wait_ge(tsum_done, i + 1)
                    nc.scalar.activation(top_ln[:], top_sum[:], ACT.Ln).then_inc(ln_done, 1)
                    act.wait_ge(shift_done, i + 1)
                    act.wait_ge(rest_done, i + 1)
                    if behind:
                        act.wait_ge(wlag_done, i)
                    for j in range(8):
                        probs = nc.scalar.activation(corr_e[:, j, :], b_corr[:, j * L:(j + 1) * L], ACT.Exp, bias=neg_shift[:, j:j + 1])
                    probs.then_inc(corre_done, 1)
                if ffn and norm and not ahead:
                    normalise_x1(i - 2, par, i - 1, False)
                if is_step(i, 0):
                    act.wait_ge(params_in, PARAMS)
                if is_step(i, 0) or is_step(i, 1):
                    half = slice(i * CHUNKS // 2, (i + 1) * CHUNKS // 2)
                    nc.scalar.activation(param_hi[:, half, :], params[:, half, :], ACT.Identity).then_inc(param_hi_done, 1)
                if is_step(i, 2):
                    nc.scalar.activation(lora_hi[:], w_b[:], ACT.Identity).then_inc(param_hi_done, 1)
                if group is not None and par == 0 and not ahead:
                    gate_exp(group)
                if ffn:
                    act.wait_ge(main_mm, i - 2)
                    nc.scalar.activation(main_g[:, FIRST:D], b_main[:, 0:COLS], ACT.Copy, scale=gate_t[:, 1:2]).then_inc(main_ev, 1)
                if group is not None and par == 0 and ahead:
                    gate_exp(group)

            run_steps(act, step)
            gate_exp(GROUPS - 1)

            for g in range(LORA_GROUPS):
                act.wait_ge(scaled_turned, g + 1)
                nc.scalar.activation(scaled_hi[:, g * LORA_GROUP * P:(g + 1) * LORA_GROUP * P], b_scaled[g][:], ACT.Identity).then_inc(scaled_hi_done, 1)

        @block.vector
        def _(dve):
            def stats(i, par, k, free):
                dve.wait_ge(x_in[par], k)
                if free is not None:
                    dve.wait_ge(nmr_done, free)
                held(0)
                nc.vector.bn_stats(bn[:, par, :], at(x_all, i)).then_inc(bn_done, 1)
                dve.wait_ge(bn_done, i + 1)
                held(1)
                nc.vector.bn_aggr(mv[:, par, :], bn[:, par, :]).then_inc(mv_done, 1)

            def gate_stats(group):
                dve.wait_ge(hidden_done, group + 1)
                held(5)
                for j in range(GROUP):
                    ins = nc.vector.bn_stats(bn_h[:, j, :], h[:, j, :])
                ins.then_inc(bn_h_done, 1)
                dve.wait_ge(bn_h_done, group + 1)
                held(6)
                for j in range(GROUP):
                    ins = nc.vector.bn_aggr(mv_h[:, j, :], bn_h[:, j, :])
                ins.then_inc(gvar_ready, 1)

            def group_tiles(group):
                return slice(group * GROUP, (group + 1) * GROUP) if isinstance(group, int) else bass.ds(group * GROUP, GROUP)

            def link(group, k, ins):
                ins.then_inc(choose_chain, 1)
                dve.wait_ge(choose_chain, group * LINKS + k)

            both = [P, GROUP, 2, E]

            def gates(group):
                if isinstance(group, int) and group == GROUPS - 1:
                    full = [P, GROUP, E, G1]
                    dve.wait_ge(gate_norm_chain, group * GATE_LINKS + GATE_LINKS - 1)
                    dve.wait_ge(gexp_done, group)
                    nc.vector.tensor_scalar(h[:], h[:], 0.0, None, ALU.max).then_inc(relu_done, 1)
                    dve.wait_ge(relu_done, 1)
                    nc.vector.tensor_tensor(gprod[:], h[:].unsqueeze(2).broadcast_to(full),
                                            gw2_b[:].unsqueeze(1).broadcast_to(full), ALU.mult).then_inc(gprod_done, 1)
                dve.wait_ge(gprod_done, group + 1)
                nc.vector.tensor_reduce(gate[:], gprod[:], AX_X, ALU.add).then_inc(gate_sum_done, 1)
                dve.wait_ge(gate_sum_done, group + 2)
                link(group, 1, nc.vector.tensor_tensor(gate[:], gate[:], gb2_b[:].unsqueeze(1).broadcast_to([P, GROUP, E]), ALU.add))

            def largest_gates(group):
                held(7)
                for j in range(GROUP):
                    ins = nc.vector.max(best[:, j, :], gate[:, j, :])
                link(group, 2, ins)
                nc.vector.tensor_tensor(gate_diff[:], best[:, :, 1], best[:, :, 0], ALU.subtract).then_inc(gdiff_ready, 1)

            def choose(group):
                for j in range(GROUP):
                    ins = nc.vector.max_index(best_at[:, j, :], best[:, j, :], gate[:, j, :])
                link(group, 3, ins)
                link(group, 4, nc.vector.tensor_tensor(onehot[:, group_tiles(group), :, :], best_at[:, :, 0:2].unsqueeze(3).broadcast_to(both),
                                                       index_b[:].unsqueeze(1).unsqueeze(1).broadcast_to(both), ALU.is_equal))

            def stats_x1(i, par):
                dve.wait_ge(x1_done, i - 1)
                if not is_step(i, 2) and not is_step(i, 3):
                    dve.wait_ge(nmr_x1_done, i - 3)
                held(3)
                nc.vector.bn_stats(bn_x1[:, par, :], at(x_all, i - 2)).then_inc(bn_x1_done, 1)
                dve.wait_ge(bn_x1_done, i - 1)
                held(4)
                nc.vector.bn_aggr(mv_x1[:, par, :], bn_x1[:, par, :]).then_inc(mv_x1_done, 1)

            def weights_low(i, behind):
                if behind:
                    dve.wait_ge(w_hi_done, i)
                    if not is_step(i, 1):
                        dve.wait_ge(wo_mm, i - 1)
                    nc.vector.tensor_tensor(w_lo[:], b_turn[:], w_hi[:], ALU.subtract).then_inc(w_lo_done, 1)

            def q_products(i, par, ahead, behind):
                if ahead:
                    dve.wait_ge(q_mm, i + 1)
                    dve.wait_ge(even_ev, i * 2 + 1)
                    if behind:
                        dve.wait_ge(corr_mm, i)
                    nc.vector.tensor_tensor(prod_q[:, 0, :], b_q[:], v_even[:, par, :], ALU.mult).then_inc(prod_q_done, 1)
                    dve.wait_ge(even_ev, i * 2 + 2)
                    nc.vector.tensor_tensor(prod_q[:, 1, :], b_q[:], v_even_sw[:, par, :], ALU.mult).then_inc(prod_q_done, 1)

            def step(i, par, ahead, behind, norm, ffn, group):
                if norm:
                    dve.wait_ge(out_mm, i - 1)
                    nc.vector.scalar_tensor_tensor(out=at(x_all, i - 2), in0=b_out[:], scalar=gate_t[:, 0:1], in1=at(x_all, i - 2),
                                                   op0=ALU.mult, op1=ALU.add).then_inc(x1_done, 1)
                    if not behind:
                        stats_x1(i, par)
                if ffn:
                    weights_low(i, behind)
                    q_products(i, par, ahead, behind)
                else:
                    q_products(i, par, ahead, behind)
                    weights_low(i, behind)
                if ahead and not is_step(i, TILES - 1):
                    stats(i + 1, 1 - par, ((i + 1) // 2 + 1) * 16 if isinstance(i, int) else (i + (2 + par)) * 8,
                          i if behind else None)
                if ffn:
                    dve.wait_ge(x_hi_done, i - 2)
                    if not is_step(i, 3):
                        dve.wait_ge(main_mm, i - 3)
                    nc.vector.tensor_tensor(x_lo[:], b_xt[:], x_hi[:], ALU.subtract).then_inc(x_lo_done, 1)
                if behind:
                    dve.wait_ge(we_mm, i)
                    dve.wait_ge(even_ev, i * 2)
                    if not is_step(i, 1):
                        dve.wait_ge(out_mm, i - 1)
                    nc.vector.tensor_tensor(prod_w[:, 0, :], b_we[:], v_even[:, 1 - par, :], ALU.mult).then_inc(prod_even_done, 1)
                    nc.vector.tensor_tensor(prod_w[:, 1, :], b_we[:], v_even_sw[:, 1 - par, :], ALU.mult).then_inc(prod_even_done, 1)
                    dve.wait_ge(wo_ev, i)
                    dve.wait_ge(odd_ev, i * 2 - 1)
                    nc.vector.tensor_tensor(prod_w[:, 2, :], b_wo[:], v_odd[:, 1 - par, :], ALU.mult).then_inc(prod_odd_done, 1)
                if ahead:
                    dve.wait_ge(corr_mm, i + 1)
                    held(2)
                    corr = b_corr[:].rearrange("p (j l) -> p j l", l=L)
                    for j in range(8):
                        largest = nc.vector.max(top[:, j, :], corr[:, j, :])
                    largest.then_inc(top_done, 1)
                    dve.wait_ge(top_done, i + 1)
                    if behind:
                        dve.wait_ge(tope_done, i)
                    nc.vector.tensor_tensor(top_d[:], top[:], top[:, :, 0:1].broadcast_to([P, 8, 8]), ALU.subtract).then_inc(topd_done, 1)
                    for j in range(8):
                        repl = nc.vector.match_replace(out=rest[:, j, :], in_to_replace=top[:, j, :], in_values=corr[:, j, :], imm_value=LOW)
                    repl.then_inc(rest_done, 1)
                    dve.wait_ge(tope_done, i + 1)
                    nc.vector.tensor_reduce(top_sum[:], top_e[:], AX_X, ALU.add).then_inc(tsum_done, 1)
                if ahead:
                    dve.wait_ge(ln_done, i + 1)
                    nc.vector.scalar_tensor_tensor(out=neg_shift[:], in0=top[:, :, 0], scalar=-1.0, in1=top_ln[:],
                                                   op0=ALU.mult, op1=ALU.subtract).then_inc(shift_done, 1)
                if norm and behind:
                    stats_x1(i, par)
                if group is not None and par == 1:
                    gate_stats(group)
                if group is not None and par == 0:
                    gates(group)
                    largest_gates(group)
                if ahead:
                    dve.wait_ge(rest_done, i + 1)
                    dve.wait_ge(corre_done, i + 1)
                    if behind:
                        dve.wait_ge(turn_mm, i)
                    nc.vector.scalar_tensor_tensor(out=w_lag[:], in0=rest[:], scalar=LOW, in1=corr_e[:],
                                                   op0=ALU.is_equal, op1=ALU.mult).then_inc(wlag_done, 1)
                if group is not None and par == 0:
                    choose(group)

            nc.vector.memset(gate[:], 0.0).then_inc(gate_sum_done, 1)
            stats(0, 0, 16, None)
            dve.wait_ge(mat_hi_done, 1)
            nc.vector.tensor_tensor(mat_lo[:], mat[:, 0:SPLIT, :], mat_hi[:], ALU.subtract).then_inc(mat_lo_done, 1)
            dve.wait_ge(tanh_done, 1)
            nc.vector.tensor_scalar(gate_r[:], gate_t[:, 1:2], 1.0 / R, None, ALU.mult).then_inc(gate_r_done, 1)
            run_steps(dve, step)
            gate_stats(GROUPS - 1)
            gates(GROUPS - 1)
            largest_gates(GROUPS - 1)
            choose(GROUPS - 1)

            dve.wait_ge(choose_chain, GROUPS * LINKS)
            nc.vector.tensor_reduce(ohsum[:], onehot[:].rearrange("p n k e -> p k e n"), AX_X, ALU.add).then_inc(ohsum_done, 1)
            dve.wait_ge(count_mm, 1)
            nc.vector.tensor_scalar(allowed[:].rearrange("p k e -> p (k e)"), b_out[:, 0:2 * E], float(CAPACITY), None, ALU.is_le).then_inc(allowed_done, 1)
            dve.wait_ge(allowed_done, 1)
            dve.wait_ge(weigh_chain, GROUPS * LINKS + 1)
            nc.vector.tensor_tensor(weighted[:], weighted[:], allowed[:].unsqueeze(1).broadcast_to([P, TILES, 2, E]), ALU.mult).then_inc(wexp_chain, 1)
            dve.wait_ge(wexp_chain, 1)
            nc.vector.tensor_tensor(w_exp[:], weighted[:, :, 0, :], weighted[:, :, 1, :], ALU.add).then_inc(wexp_chain, 1)
            dve.wait_ge(wexp_chain, 2)
            dve.wait_ge(gate_r_done, 1)

            for g in range(LORA_GROUPS // 2):
                scale(nc.vector, g).then_inc(scaled_done, 1)

            def scaled_low(g):
                tokens = slice(g * LORA_GROUP * P, (g + 1) * LORA_GROUP * P)
                dve.wait_ge(scaled_hi_done, g + 1)
                nc.vector.tensor_tensor(scaled_lo[:, tokens], b_scaled[g][:], scaled_hi[:, tokens], ALU.subtract).then_inc(scaled_lo_done, 1)

            scaled_low(0)
            for n in range(TILES):
                if n == 0 or n == TILES - 1:
                    dve.wait_ge(base_done, TILES - 1 if n == 0 else TILES)
                dve.wait_ge(lora_mm, n + 1)
                nc.vector.scalar_tensor_tensor(out=at(ctx_all, n), in0=b_lora[n % LORA_GROUP][:], scalar=gate_r[:, 0:1],
                                               in1=at(ctx_all, n), op0=ALU.mult, op1=ALU.add).then_inc(result_done, 1)
                if n % LORA_GROUP == 1 and n // LORA_GROUP + 1 < LORA_GROUPS:
                    scaled_low(n // LORA_GROUP + 1)


def kernel(**inputs):
    import concourse.bacc as bacc
    from concourse.bass_utils import run_bass_kernel_spmd as run

    def f(name):
        return np.ascontiguousarray(inputs[name])

    arrays = {
        "x": f("x").reshape(BATCH * L, D),
        "ctx": f("ctx_4096").reshape(BATCH * L, D),
        "mats": transform_matrices(),
        "index": np.arange(E).astype(np.float32),
        "g_xattn": f("g_xattn"),
        "g_ffn": f("g_ffn"),
        "params_t": np.ascontiguousarray(np.concatenate(
            [f("L0_ffn_lora_A").transpose(1, 0, 2).reshape(D, ER), f("L0_ffn_gw1").T, f("L0_ffn_weight").T], axis=1)),
        "lora_b": f("L0_ffn_lora_B").reshape(ER, D),
        "gb1": f("L0_ffn_gb1"),
        "gamma": f("L0_ffn_ln_gamma"),
        "beta": f("L0_ffn_ln_beta"),
        "gw2": f("L0_ffn_gw2"),
        "gb2": f("L0_ffn_gb2"),
    }
    nc = bacc.Bacc("TRN2", target_bir_lowering=False, num_devices=1)
    aps = [nc.dram_tensor(f"in_{n}", a.shape, F32, kind="ExternalInput").ap() for n, a in arrays.items()]
    out = nc.dram_tensor("out_x", (BATCH * L, D), F32, kind="ExternalOutput").ap()
    build(nc, *aps, out)
    r = run(nc, [{f"in_{n}": a for n, a in arrays.items()}], core_ids=[0])
    return r.results[0]["out_x"].reshape(BATCH, L, D)
```
